# Optimizing a Trainium2 kernel written in Bass

```python
import numpy as np
import jax
import jax.numpy as jnp

def _softmax(x, axis=-1):
    return jax.nn.softmax(x, axis=axis)

def _gelu(x):
    return jax.nn.gelu(x, approximate=True)

def _silu(x):
    return jax.nn.silu(x)

def _sigmoid(x):
    return jax.nn.sigmoid(x)

def _layernorm(x, axis=-1, eps=1e-05):
    m = jnp.mean(x, axis=axis, keepdims=True)
    v = jnp.var(x, axis=axis, keepdims=True)
    return (x - m) / jnp.sqrt(v + eps)

def _scatter_add(tgt, idx, src, axis=0):
    return tgt.at[idx].add(src)

def _segment_sum(src, seg, n):
    return jax.ops.segment_sum(src, seg, n)
kernel_name = 'mk_adj_preln_d1_adj_r2_99074b'

def setup_inputs(seed: int=0):
    np.random.seed(seed)
    _w = jnp.asarray

    def _rec_inputs():
        import jax
        import jax.numpy as jnp
        _gk = jax.random.key(seed)
        x = -0.0005207 + 1.001 * jax.random.normal(jax.random.fold_in(_gk, 1), (4096, 256), jnp.float32)
        _a = jax.random.bernoulli(jax.random.fold_in(_gk, 2), 0.000488281, (4096, 4096))
        _a = jnp.logical_or(_a, jnp.swapaxes(_a, -1, -2))
        _a = jnp.logical_or(_a, jnp.eye(4096, dtype=bool))
        _af = _a.astype(jnp.float32)
        _af = _af * jax.random.uniform(jax.random.fold_in(_gk, 3), (4096, 4096), jnp.float32, 0.05, 5.41998)
        adj = _af
        return (x, adj)
    x, adj = _rec_inputs()

    def _L0_gnn_setup():
        import jax, jax.numpy as jnp
        import numpy as np
        N = 2048
        DIM_IN = 256
        DIM_Q = 256
        DIM_K = 256
        N_GRAPHS = 32
        key = jax.random.key(seed)
        ks = jax.random.split(key, 9)
        x = jax.random.normal(ks[0], (N, DIM_IN), dtype=jnp.float32)
        b = jax.random.normal(ks[1], (N, N), dtype=jnp.float32)
        edge_encoding = jax.random.normal(ks[2], (N, N), dtype=jnp.float32)
        ptr = jnp.arange(N_GRAPHS + 1, dtype=jnp.int64) * (N // N_GRAPHS)
        s_in = 1.0 / np.sqrt(DIM_IN)
        Wq = jax.random.normal(ks[3], (DIM_Q, DIM_IN), dtype=jnp.float32) * s_in
        bq = jnp.zeros((DIM_Q,), dtype=jnp.float32)
        Wk = jax.random.normal(ks[4], (DIM_K, DIM_IN), dtype=jnp.float32) * s_in
        bk = jnp.zeros((DIM_K,), dtype=jnp.float32)
        Wv = jax.random.normal(ks[5], (DIM_K, DIM_IN), dtype=jnp.float32) * s_in
        bv = jnp.zeros((DIM_K,), dtype=jnp.float32)
        return {'x': x, 'b': b, 'edge_encoding': edge_encoding, 'ptr': ptr, 'Wq': Wq, 'bq': bq, 'Wk': Wk, 'bk': bk, 'Wv': Wv, 'bv': bv}
    _L0_gnn_all = _L0_gnn_setup()
    _L0_gnn_in = {k: v for k, v in _L0_gnn_all.items() if k in ('ptr', 'Wq', 'bq', 'Wk', 'bk', 'Wv', 'bv')}
    del _L0_gnn_all
    return {'x': x, 'adj': adj, 'L0_gnn_ptr': _L0_gnn_in['ptr'], 'L0_gnn_Wq': _L0_gnn_in['Wq'], 'L0_gnn_bq': _L0_gnn_in['bq'], 'L0_gnn_Wk': _L0_gnn_in['Wk'], 'L0_gnn_bk': _L0_gnn_in['bk'], 'L0_gnn_Wv': _L0_gnn_in['Wv'], 'L0_gnn_bv': _L0_gnn_in['bv']}

def reference(x, adj, L0_gnn_ptr, L0_gnn_Wq, L0_gnn_bq, L0_gnn_Wk, L0_gnn_bk, L0_gnn_Wv, L0_gnn_bv):
    import jax
    import jax.numpy as jnp

    def _L0_gnn_ref(x, b, edge_encoding, ptr, Wq, bq, Wk, bk, Wv, bv):
        import jax, jax.numpy as jnp
        import numpy as np
        N = 2048
        DIM_IN = 256
        DIM_Q = 256
        DIM_K = 256
        N_GRAPHS = 32
        n = x.shape[0]
        graph_id = jnp.searchsorted(ptr, jnp.arange(n), side='right') - 1
        mask = graph_id[:, None] == graph_id[None, :]
        query = x @ Wq.T + bq
        key = x @ Wk.T + bk
        value = x @ Wv.T + bv
        scale = 1.0 / jnp.sqrt(jnp.float32(query.shape[-1]))
        a = jnp.where(mask, query @ key.T * scale, 0.0)
        scores = (a + b + edge_encoding) * jnp.where(mask, 1.0, -1000000.0)
        softmax = jax.nn.softmax(scores, axis=-1) * mask
        return softmax @ value
    h = jnp.maximum(_layernorm(x, axis=-1), 0.0)
    x = x + _L0_gnn_ref(h, adj, adj, L0_gnn_ptr, L0_gnn_Wq, L0_gnn_bq, L0_gnn_Wk, L0_gnn_bk, L0_gnn_Wv, L0_gnn_bv)
    return x

_drawn_inputs = setup_inputs


def setup_inputs(seed=0):
    import zlib

    import numpy as np

    out = dict(_drawn_inputs(seed))
    spreads = {'L0_gnn_bq': (0.0, 0.8), 'L0_gnn_bk': (0.0, 0.8), 'L0_gnn_bv': (0.0, 0.1)}
    factors = {}
    for name, (base, spread) in spreads.items():
        noise = np.random.default_rng([zlib.crc32(name.encode()), seed]).standard_normal(out[name].shape)
        drawn = base * np.exp(spread * noise) if base else spread * noise
        out[name] = jnp.asarray(drawn.astype(out[name].dtype))
    for name, factor in factors.items():
        out[name] = (out[name] * factor).astype(out[name].dtype)
    return out
```

```python
from contextlib import ExitStack

import concourse.bass as bass
from concourse import mybir

P = 128
BIG = 3.0e38
FAR = 1.0e30
FARTHEST = 1.5e38
OFF_SCALE = 2.0e6
EPS = 1e-5

ALU = mybir.AluOpType
ACT = mybir.ActivationFunctionType
AX = mybir.AxisListType
F32 = mybir.dt.float32
F32R = mybir.dt.float32r
I32 = mybir.dt.int32


def build_program(nc, x, adj, ptr, Wq, bq, Wk, bk, Wv, bv, out):
    N, D = x.shape
    H = N // 2
    NT = H // P
    NG = ptr.shape[0]
    GS = H // (ptr.shape[0] - 1)
    KD = D // P
    CH = 512
    NC = H // CH
    KB = CH // P
    DU = D + 1
    SC = 1.0 / float(D) ** 0.5

    with ExitStack() as ctx:
        def sb(name, shape, dt=F32, to=ctx):
            return to.enter_context(nc.sbuf_tensor(name, shape, dt))

        def ps(name):
            return ctx.enter_context(nc.psum_tensor(name, [P, 512], F32))

        def sem(name):
            return ctx.enter_context(nc.semaphore(name))

        def sem2(name):
            return [sem(name + "0"), sem(name + "1")]

        score_bank = [ps(f"score_bank{i}") for i in range(3)]
        turn_bank = [ps(f"turn_bank{i}") for i in range(2)]
        out_bank = ps("out_bank")
        m0 = ps("m0")
        m1 = ps("m1")

        x_big = sb("x_big", [P, NT + 1, D])
        x_small = sb("x_small", [P, 2, D])
        probs = sb("probs", [P, H])
        G32 = sb("G32", [P, KD, D])
        WvT = sb("WvT", [P, KD, DU])
        bias_row = sb("bias_row", [P, DU])
        c_col = sb("c_col", [P, KD])
        c_wide = sb("c_wide", [P, KD, P])
        ident = sb("ident", [P, P])
        cap = sb("cap", [P, P])
        floor = sb("floor", [P, P])
        bq_col = sb("bq_col", [P, KD])
        bk_col = sb("bk_col", [P, KD])
        half = sb("half", [P, 1])
        W_sb = probs[:, 0:3 * KD * D].rearrange("p (w c d) -> p w c d", w=3, c=KD)
        Wq_sb, Wk_sb, Wv_sb = W_sb[:, 0], W_sb[:, 1], W_sb[:, 2]
        bq_wide = probs[:, 3 * KD * D:3 * KD * D + KD * P].rearrange("p (c d) -> p c d", c=KD)
        ptr_row = sb("ptr_row", [P, NG], I32)
        ptr_drawn = sb("ptr_drawn", [P, NG], I32)
        ptr_same = sb("ptr_same", [P, NG])
        path = sb("path", [P, 1], I32)
        moments = sb("moments", [P, 2, 6])
        mean_var = sb("mean_var", [P, 2, 2])
        var_eps = sb("var_eps", [P, 2])
        rstd = sb("rstd", [P, 2])
        xn = sb("xn", [P, 2, D])
        hT = sb("hT", [P, 2, KD, P])
        V32 = sb("V32", [P, 2, DU])
        Qs = sb("Qs", [P, 2, KD, P])
        out_s = sb("out_s", [P, 2, D])

        with ExitStack() as regular:
            adj_big = [sb(f"adj_big{i}", [P, N], to=regular) for i in range(2)]
            adj_small = [sb(f"adj_small{i}", [P, N], to=regular) for i in range(2)]
            hT_hi = sb("hT_hi", [P, KD, H], F32R, to=regular)
            hT_lo = sb("hT_lo", [P, KD, H], F32R, to=regular)
            V_hi = sb("V_hi", [P, NT, D], F32R, to=regular)
            V_lo = sb("V_lo", [P, NT, D], F32R, to=regular)
            u_big = sb("u_big", [P, NT], to=regular)
            PT32 = sb("PT32", [P, 2, CH], to=regular)
            PT_hi = sb("PT_hi", [P, NC, CH], F32R, to=regular)
            PT_lo = sb("PT_lo", [P, NC, CH], F32R, to=regular)
            G_hi = sb("G_hi", [P, KD, D], F32R, to=regular)
            G_lo = sb("G_lo", [P, KD, D], F32R, to=regular)
            Qb32 = sb("Qb32", [P, KD, P], to=regular)
            Qb_hi = sb("Qb_hi", [P, 2, KD, P], F32R, to=regular)
            Qb_lo = sb("Qb_lo", [P, 2, KD, P], F32R, to=regular)
            diag = sb("diag", [P, 2, P], to=regular)
            PsT = sb("PsT", [P, 2, P], to=regular)
            off_min = sb("off_min", [P, 2, 2], to=regular)
            bound_s = sb("bound_s", [P, 2, 3], to=regular)
            bound_b = sb("bound_b", [P, 2, 7], to=regular)
            sum_s = sb("sum_s", [P, 2, 4], to=regular)
            sum_b = sb("sum_b", [P, 2, 5], to=regular)
            out_b = sb("out_b", [P, 2, D], to=regular)

        with ExitStack() as general:
            g_hT = sb("g_hT", [P, KD, N], to=general)
            g_V = sb("g_V", [P, N // P, DU], to=general)
            g_graph = sb("g_graph", [P, N], to=general)
            g_adj = sb("g_adj", [P, N], to=general)
            g_in = sb("g_in", [P, N], to=general)
            g_z = sb("g_z", [P, N], to=general)
            g_rows = sb("g_rows", [P, N // P], to=general)
            g_row_id = sb("g_row_id", [P, N // P], I32, to=general)
            g_ptr = sb("g_ptr", [P, NG], to=general)
            g_row = sb("g_row", [P, 3], to=general)
            g_sum = sb("g_sum", [P, 2], to=general)
            g_key_id = g_z[:].bitcast(I32)

        w_in = sem("w_in")
        x_in = [sem(f"x_in{i}") for i in range(5)]
        ptr_in = sem("ptr_in")
        ptr_id = sem("ptr_id")
        ptr_step = sem("ptr_step")
        path_known = sem("path_known")
        w_wide = sem("w_wide")
        const_ready = sem("const_ready")
        ident_ready = sem("ident_ready")
        prep_psum = sem("prep_psum")
        prep_done = sem("prep_done")
        G_step = sem("G_step")
        moments_done = sem2("moments_done")
        mean_done = sem2("mean_done")
        var_ready = sem2("var_ready")
        rstd_ready = sem2("rstd_ready")
        xn_ready = sem2("xn_ready")
        p_turned = sem2("p_turned")
        p_h32 = sem2("p_h32")
        p_hi = sem2("p_hi")
        p_lo = sem2("p_lo")
        p_vpsum = sem2("p_vpsum")
        p_v32 = sem2("p_v32")
        p_vhi = sem2("p_vhi")
        p_vlo = sem2("p_vlo")
        adj_b_in = sem2("adj_b_in")
        adj_s_in = sem2("adj_s_in")
        x_s_in = sem2("x_s_in")
        adj_b_free = sem2("adj_b_free")
        adj_s_free = sem2("adj_s_free")
        s_turned = sem2("s_turned")
        s_hT = sem2("s_hT")
        s_qpsum = sem2("s_qpsum")
        s_vpsum = sem2("s_vpsum")
        s_q = sem2("s_q")
        s_v = sem2("s_v")
        s_spsum = sem2("s_spsum")
        s_diag = sem2("s_diag")
        s_masked = sem2("s_masked")
        s_off = sem2("s_off")
        s_offu = sem2("s_offu")
        s_bound = sem2("s_bound")
        s_stat = sem2("s_stat")
        s_probs = sem2("s_probs")
        s_outside = sem2("s_outside")
        s_tpsum = sem2("s_tpsum")
        s_pT = sem2("s_pT")
        s_opsum = sem2("s_opsum")
        s_total = sem2("s_total")
        s_recip = sem2("s_recip")
        s_out = sem2("s_out")
        s_stored = sem2("s_stored")
        b_qpsum = sem2("b_qpsum")
        b_q32 = sem2("b_q32")
        b_qhi = sem2("b_qhi")
        b_q = sem2("b_q")
        b_off = sem2("b_off")
        b_offu = sem2("b_offu")
        b_spsum = sem2("b_spsum")
        b_scores = sem2("b_scores")
        b_stat = sem2("b_stat")
        b_probs = sem2("b_probs")
        b_tpsum = sem2("b_tpsum")
        b_pT32 = sem2("b_pT32")
        b_pThi = sem2("b_pThi")
        b_pT = sem2("b_pT")
        b_pv = sem2("b_pv")
        b_total = sem2("b_total")
        b_recip = sem2("b_recip")
        b_out = sem2("b_out")
        b_stored = sem2("b_stored")

        g_ids = sem("g_ids")
        g_graphs = sem("g_graphs")
        g_adj_in = sem("g_adj_in")
        g_step = sem("g_step")
        g_exp = sem("g_exp")
        g_spsum = sem("g_spsum")
        g_tpsum = sem("g_tpsum")
        g_turned = sem("g_turned")
        g_opsum = sem("g_opsum")
        g_out = sem("g_out")
        g_stored = sem("g_stored")
        g_x_in = sem("g_x_in")

        LAST = NT // 2 - 1
        GC_STEPS = N // CH
        G_BOUND = GC_STEPS + 9
        G_STEPS = G_BOUND + 4
        GT = N // P
        GC = N // CH

        def regular_ptr(eng):
            eng.wait_ge(path_known, 1)
            return eng.value_load(path[0:1, 0:1], min_val=0, max_val=1) == 1

        def fixed(eng, value):
            return value if isinstance(value, int) else eng.to_reg(value)

        def pairs(eng, body):
            body(0, 0, None, 0)
            with eng.Fori(0, LAST) as it:
                body(it, 1, it, it + 1)
                body(it + 1, 0, it, it + 1)
            body(LAST, 1, LAST, None)

        block = ctx.enter_context(nc.Block())

        @block.sync
        def _(sp):
            sp.dma_start(ptr_row[:], ptr.rearrange("(a d) -> a d", a=1).broadcast_to([P, NG])
                         ).then_inc(ptr_in, 16)
            for w, dst in ((Wq, Wq_sb), (Wk, Wk_sb), (Wv, Wv_sb)):
                sp.dma_start(dst, w.rearrange("(c p) d -> p c d", p=P)).then_inc(w_in, 16)
            sp.dma_start(bq_col[:], bq.rearrange("(c p) -> p c", p=P),
                         allow_slow_non_contiguous=True).then_inc(w_in, 16)
            sp.dma_start(bk_col[:], bk.rearrange("(c p) -> p c", p=P),
                         allow_slow_non_contiguous=True).then_inc(w_in, 16)
            sp.dma_start(bias_row[:, 0:D], bv.rearrange("(a d) -> a d", a=1).broadcast_to([P, D])
                         ).then_inc(w_in, 16)
            Q4 = NT // 4
            for i in range(4):
                rows = x[H + i * Q4 * P:H + (i + 1) * Q4 * P, :]
                sp.dma_start(x_big[:, i * Q4:(i + 1) * Q4, :],
                             rows.rearrange("(t p) d -> p t d", p=P)).then_inc(x_in[i], 16)
            sp.dma_start(x_big[:, NT, :], x[0:P, :]).then_inc(x_in[4], 16)

            with sp.If(regular_ptr(sp)):
                def load(u, q):
                    n = u * 2 + q
                    sp.wait_ge(s_out[q], u + 1)
                    sp.dma_start(x_small[:, q, :], x[bass.ds(n * P, P), :]).then_inc(x_s_in[q], 16)
                    sp.wait_ge(adj_s_free[q], u + 1)
                    sp.dma_start(adj_small[q][:], adj[bass.ds(n * P, P), :]).then_inc(adj_s_in[q], 16)
                    sp.wait_ge(adj_b_free[q], u + 1)
                    sp.dma_start(adj_big[q][:], adj[bass.ds(n * P + H, P), :]).then_inc(adj_b_in[q], 16)

                with sp.Fori(0, NT // 2) as u:
                    load(u, 0)
                    load(u, 1)
            with sp.Else():
                def g_rows_of(a, t):
                    return a[bass.ds(t * P, P), :]

                sp.dma_start(x_small[:, 0, :], g_rows_of(x, 0)).then_inc(x_s_in[0], 16)
                with sp.Fori(1, GT) as t:
                    sp.wait_ge(xn_ready[0], t)
                    sp.dma_start(x_small[:, 0, :], g_rows_of(x, t)).then_inc(x_s_in[0], 16)
                sp.wait_ge(g_graphs, 1)
                sp.dma_start(g_adj[:], g_rows_of(adj, 0)).then_inc(g_adj_in, 16)
                sp.dma_start(x_small[:, 1, :], g_rows_of(x, 0)).then_inc(g_x_in, 16)
                with sp.Fori(1, GT) as t:
                    sp.wait_ge(g_out, t)
                    sp.dma_start(g_rows_of(out, t - 1), out_s[:, 0, :]).then_inc(g_stored, 16)
                    sp.wait_ge(g_stored, t * 16)
                    sp.dma_start(g_adj[:], g_rows_of(adj, t)).then_inc(g_adj_in, 16)
                    sp.dma_start(x_small[:, 1, :], g_rows_of(x, t)).then_inc(g_x_in, 16)
                sp.wait_ge(g_out, GT)
                sp.dma_start(g_rows_of(out, GT - 1), out_s[:, 0, :]).then_inc(g_stored, 16)
                sp.wait_ge(g_stored, GT * 16)

        @block.scalar
        def _(act):
            for q in range(2):
                act.sem_inc(adj_s_free[q], 1)
                act.sem_inc(adj_b_free[q], 1)
            act.wait_ge(prep_psum, 1)
            act.activation(G32[:].rearrange("p c d -> p (c d)"), m0[:, 0:KD * D], ACT.Copy,
                           scale=SC / 2).then_inc(prep_done, 1)
            act.wait_ge(prep_psum, 2)
            act.activation(WvT[:, :, 0:D], m1[:, 0:KD * D].rearrange("p (c d) -> p c d", c=KD),
                           ACT.Copy).then_inc(prep_done, 1)

            with act.If(regular_ptr(act)):
                def turn_in(u, q):
                    act.wait_ge(p_turned[q], u + 1)
                    src = score_bank[q][:, 0:D]
                    act.activation(hT[:, q].rearrange("p c d -> p (c d)"), src, ACT.Relu
                                   ).then_inc(p_h32[q], 1)
                    act.activation(hT_hi[:, :, bass.ds((u * 2 + q) * P, P)],
                                   src.rearrange("p (c d) -> p c d", c=KD), ACT.Relu).then_inc(p_hi[q], 1)

                def value_hi(u, q):
                    tiles = fixed(act, u + 2)
                    act.wait_ge(prep_done, 2)
                    act.wait_ge(p_v32[q], tiles)
                    act.activation(V_hi[:, u * 2 + q, :], V32[:, q, 0:D], ACT.Copy).then_inc(p_vhi[q], 1)

                with act.Fori(0, NT // 2) as u:
                    for q in range(2):
                        turn_in(u, q)
                        value_hi(u, q)

                def q_big(u, q):
                    act.wait_ge(b_qpsum[q], u + 1)
                    for c in range(KD):
                        last = act.activation(Qb32[:, c, :], m1[:, c * P:(c + 1) * P], ACT.Identity,
                                              bias=c_col[:, c:c + 1])
                    last.then_inc(b_q32[q], 1)

                q_big(0, 0)

                def body(u, q, up, un):
                    act.wait_ge(s_turned[q], u + 1)
                    act.activation(hT[:, q].rearrange("p c d -> p (c d)"), m0[:, 0:D], ACT.Relu
                                   ).then_inc(s_hT[q], 1)
                    act.wait_ge(s_stat[q], u + 1)
                    act.activation(diag[:, q, :], diag[:, q, :], ACT.Exp, bias=bound_s[:, q, 1:2],
                                   scale=-1.0, accum_out=sum_s[:, q, 0:1]).then_inc(s_probs[q], 1)
                    act.activation(adj_small[q][:], adj_small[q][:], ACT.Exp, bias=bound_s[:, q, 2:3],
                                   scale=-1.0, accum_out=sum_s[:, q, 1:2]).then_inc(adj_s_free[q], 1)
                    act.wait_ge(s_tpsum[q], u + 1)
                    act.copy(PsT[:, q, :], m1[:, 0:P]).then_inc(s_pT[q], 1)
                    act.wait_ge(b_stat[q], u + 1)
                    for i in range(2):
                        act.activation(probs[:, i * H // 2:(i + 1) * H // 2],
                                       adj_big[q][:, H + i * H // 2:H + (i + 1) * H // 2], ACT.Exp,
                                       bias=bound_b[:, q, 5:6], scale=-1.0,
                                       accum_out=sum_b[:, q, i:i + 1]).then_inc(b_probs[q], 1)
                    for c in range(NC):
                        act.wait_ge(b_tpsum[q], u * NC + (c + 1))
                        if c >= 2:
                            act.wait_ge(b_pT[q], u * NC + (c - 1))
                        elif up is not None:
                            act.wait_ge(b_pT[1 - q], up * NC + (c + 3))
                        act.copy(PT32[:, c % 2, :], turn_bank[c % 2][:]).then_inc(b_pT32[q], 1)
                    act.activation(adj_big[q][:, 0:H], adj_big[q][:, 0:H], ACT.Exp,
                                   bias=bound_b[:, q, 6:7], scale=-1.0,
                                   accum_out=sum_b[:, q, 2:3]).then_inc(adj_b_free[q], 1)
                    if un is not None:
                        q_big(un, 1 - q)
                    n = u * 2 + q
                    act.wait_ge(s_out[q], u + 2)
                    act.dma_start(out[bass.ds(n * P, P), :], out_s[:, q, :]).then_inc(s_stored[q], 16)
                    if up is not None:
                        store_big(up, 1 - q)

                def store_big(u, q):
                    act.wait_ge(b_out[q], u + 1)
                    act.dma_start(out[bass.ds((u * 2 + q) * P + H, P), :], out_b[:, q, :]
                                  ).then_inc(b_stored[q], 16)

                pairs(act, body)
                store_big(LAST, 1)
                for q in range(2):
                    act.wait_ge(s_stored[q], 16 * (NT // 2 + 1))
                    act.wait_ge(b_stored[q], 16 * (NT // 2 + 1))
            with act.Else():
                with act.Fori(0, GT) as t:
                    act.wait_ge(s_turned[0], t + 1)
                    act.activation(hT[:, 0].rearrange("p c d -> p (c d)"), m0[:, 0:D], ACT.Relu)
                    act.activation(g_hT[:, :, bass.ds(t * P, P)],
                                   m0[:, 0:D].rearrange("p (c d) -> p c d", c=KD), ACT.Relu
                                   ).then_inc(s_hT[0], 1)
                with act.Fori(0, GT) as t:
                    act.wait_ge(g_step, t * G_STEPS + G_BOUND)
                    act.activation(g_z[:], g_z[:], ACT.Exp, bias=g_row[:, 2:3], scale=-1.0,
                                   accum_out=g_sum[:, 0:1]).then_inc(g_exp, 1)
                    for c in range(GC):
                        act.wait_ge(g_tpsum, t * GC + (c + 1))
                        act.copy(g_adj[:, c * CH:(c + 1) * CH], turn_bank[c % 2][:]
                                 ).then_inc(g_turned, 1)

        @block.gpsimd
        def _(pool):
            for q in range(2):
                pool.sem_inc(p_vlo[q], 1)
            pool.memset(ident[:], 0.0).then_inc(ident_ready, 1)
            pool.wait_ge(ident_ready, 1)
            pool.affine_select(out=ident[:], in_=ident[:], compare_op=ALU.not_equal, fill=1.0, base=0,
                               pattern=[[-1, P]], channel_multiplier=1).then_inc(ident_ready, 1)
            pool.memset(half[:], -0.5).then_inc(ident_ready, 1)
            pool.wait_ge(ident_ready, 3)
            pool.iota(ptr_drawn[:], pattern=[[GS, NG]], base=0, channel_multiplier=0
                      ).then_inc(ptr_id, 1)

            def root(count, q):
                pool.wait_ge(var_ready[q], count)
                pool.tensor_tensor(rstd[:, q:q + 1], var_eps[:, q:q + 1], half[:, 0:1], ALU.pow
                                   ).then_inc(rstd_ready[q], 1)

            with pool.If(regular_ptr(pool)):
                def value_lo(u, q):
                    n = u * 2 + q
                    pool.wait_ge(p_vhi[q], u + 1)
                    pool.tensor_tensor(V_lo[:, n, :], V32[:, q, 0:D], V_hi[:, n, :].bitcast(F32),
                                       ALU.subtract)
                    pool.tensor_copy(u_big[:, bass.ds(n, 1)], V32[:, q, D:DU]).then_inc(p_vlo[q], 1)

                root(1, 0)
                with pool.Fori(0, NT // 2) as u:
                    root(u + 1, 1)
                    value_lo(u, 0)
                    root(u + 2, 0)
                    value_lo(u, 1)

                def q_split(u, q):
                    tiles = fixed(pool, u + 1)
                    pool.wait_ge(ident_ready, 3)
                    pool.wait_ge(b_q32[q], tiles)
                    pool.tensor_scalar(Qb_hi[:, q], Qb32[:], 1.0, 0.0, ALU.mult, ALU.add
                                       ).then_inc(b_qhi[q], 1)
                    pool.wait_ge(b_qhi[q], u + 1)
                    pool.tensor_tensor(Qb_lo[:, q], Qb32[:], Qb_hi[:, q].bitcast(F32), ALU.subtract
                                       ).then_inc(b_q[q], 1)

                q_split(0, 0)

                def body(u, q, up, un):
                    if un is not None:
                        root(un + (NT // 2 + 1), 1 - q)
                    for c in range(NC):
                        chunks = fixed(pool, u * NC + (c + 1))
                        used = None if up is None else fixed(pool, up * NC + (c + 1))
                        pool.wait_ge(ident_ready, 3)
                        pool.wait_ge(b_pT32[q], chunks)
                        if up is not None:
                            pool.wait_ge(b_pv[1 - q], used)
                        pool.tensor_scalar(PT_hi[:, c, :], PT32[:, c % 2, :], 1.0, 0.0, ALU.mult, ALU.add
                                           ).then_inc(b_pThi[q], 1)
                        pool.wait_ge(b_pThi[q], u * NC + (c + 1))
                        pool.tensor_tensor(PT_lo[:, c, :], PT32[:, c % 2, :], PT_hi[:, c, :].bitcast(F32),
                                           ALU.subtract).then_inc(b_pT[q], 1)
                        if c == NC - 1 and un is not None:
                            q_split(un, 1 - q)

                pairs(pool, body)
            with pool.Else():
                pool.iota(g_key_id, pattern=[[1, N]], base=0, channel_multiplier=0).then_inc(g_ids, 1)
                pool.iota(g_row_id[:], pattern=[[P, GT]], base=0, channel_multiplier=1
                          ).then_inc(g_ids, 1)
                with pool.Fori(0, GT) as t:
                    root(t + 1, 0)

        @block.vector
        def _(dve):
            for q in range(2):
                dve.sem_inc(p_lo[q], 1)
                dve.sem_inc(p_v32[q], 1)
                dve.sem_inc(s_out[q], 1)
                dve.sem_inc(s_stored[q], 16)
                dve.sem_inc(b_stored[q], 16)
            dve.wait_ge(ptr_in, 16)
            dve.wait_ge(ptr_id, 1)
            dve.tensor_tensor(ptr_same[:], ptr_row[:], ptr_drawn[:], ALU.is_equal).then_inc(ptr_step, 1)
            dve.wait_ge(ptr_step, 1)
            dve.tensor_reduce(path[:], ptr_same[:], AX.X, ALU.min).then_inc(path_known, 1)
            dve.memset(cap[:], -FAR).then_inc(const_ready, 1)
            dve.memset(floor[:], -BIG).then_inc(const_ready, 1)
            dve.wait_ge(const_ready, 2)
            for g in range(P // GS):
                s = slice(g * GS, (g + 1) * GS)
                dve.memset(cap[s, s], BIG)
                last = dve.memset(floor[s, s], FAR)
            last.then_inc(const_ready, 1)
            dve.wait_ge(const_ready, 3)
            dve.wait_ge(w_in, 6 * 16)
            for c in range(KD):
                last = dve.tensor_scalar(bq_wide[:, c, :], cap[:], 0.0, bq_col[:, c:c + 1], ALU.mult,
                                         ALU.add)
            last.then_inc(w_wide, 1)
            dve.wait_ge(prep_psum, 3)
            dve.tensor_scalar(c_col[:], out_bank[:, 0:KD], SC / 2, None, ALU.mult).then_inc(G_step, 1)
            dve.tensor_scalar(WvT[:, :, D], out_bank[:, KD:2 * KD], SC, None, ALU.mult)
            dve.tensor_scalar(bias_row[:, D:DU], out_bank[:, 2 * KD:2 * KD + 1], SC, None, ALU.mult
                              ).then_inc(prep_done, 1)
            dve.wait_ge(G_step, 1)
            for c in range(KD):
                last = dve.tensor_scalar(c_wide[:, c, :], cap[:], 0.0, c_col[:, c:c + 1], ALU.mult,
                                         ALU.add)
            def statistics(src, count, q):
                dve.bn_stats(moments[:, q, :], src).then_inc(moments_done[q], 1)
                count = fixed(dve, count)
                dve.wait_ge(const_ready, 3)
                dve.wait_ge(moments_done[q], count)
                dve.bn_aggr(mean_var[:, q, :], moments[:, q, :]).then_inc(mean_done[q], 1)
                dve.wait_ge(mean_done[q], count)
                dve.tensor_scalar(var_eps[:, q:q + 1], mean_var[:, q, 1:2], EPS, None, ALU.add
                                  ).then_inc(var_ready[q], 1)

            def normalize(src, count, q):
                dve.wait_ge(rstd_ready[q], count)
                dve.tensor_scalar(xn[:, q, :], src, mean_var[:, q, 0:1], rstd[:, q:q + 1],
                                  ALU.subtract, ALU.mult).then_inc(xn_ready[q], 1)

            with dve.If(regular_ptr(dve)):
                dve.wait_ge(prep_done, 3)
                dve.tensor_copy(G_hi[:], G32[:]).then_inc(G_step, 1)
                dve.wait_ge(G_step, 2)
                dve.tensor_tensor(G_lo[:], G32[:], G_hi[:].bitcast(F32), ALU.subtract).then_inc(G_step, 1)
                for i in range(4):
                    dve.wait_ge(x_in[i], 16)
                dve.wait_ge(x_in[4], 16)
                statistics(x_big[:, 0, :], 1, 0)
                normalize(x_big[:, 0, :], 1, 0)

                def prelude(u, q, nxt):
                    n = u * 2 + q
                    statistics(x_big[:, n + 1, :], nxt, 1 - q)
                    dve.wait_ge(p_hi[q], u + 1)
                    at = bass.ds(n * P, P)
                    dve.scalar_tensor_tensor(out=hT_lo[:, :, at],
                                             in0=score_bank[q][:, 0:D].rearrange("p (c d) -> p c d", c=KD),
                                             scalar=0.0, in1=hT_hi[:, :, at].bitcast(F32),
                                             op0=ALU.max, op1=ALU.subtract).then_inc(p_lo[q], 1)
                    dve.wait_ge(p_vlo[q], u + 1)
                    dve.wait_ge(p_vpsum[q], u + 1)
                    dve.tensor_tensor(V32[:, q, :], turn_bank[q][:, 0:DU], bias_row[:], ALU.add
                                      ).then_inc(p_v32[q], 1)
                    normalize(x_big[:, n + 1, :], nxt, 1 - q)

                with dve.Fori(0, NT // 2) as u:
                    prelude(u, 0, u + 1)
                    prelude(u, 1, u + 2)

                def off_big(u, q):
                    dve.wait_ge(adj_b_in[q], u * 16 + 16)
                    dve.tensor_scalar(adj_big[q][:, 0:H], adj_big[q][:, 0:H], OFF_SCALE, None, ALU.mult,
                                      ALU.min, accum_out=bound_b[:, q, 0:1]).then_inc(b_off[q], 1)
                    dve.wait_ge(b_off[q], u + 1)
                    dve.tensor_tensor(bound_b[:, q, 1:2], bound_b[:, q, 0:1],
                                      u_big[:, bass.ds(u * 2 + q, 1)], ALU.add).then_inc(b_offu[q], 1)

                dve.wait_ge(p_vlo[1], NT // 2 + 1)
                off_big(0, 0)

                def scores(u, q, c):
                    products = fixed(dve, u * NC + (c + 1))
                    before = fixed(dve, u + 1 if c == 0 else u * NC + c)
                    dve.wait_ge(const_ready, 3)
                    dve.wait_ge(b_spsum[q], products)
                    dve.wait_ge(b_offu[q] if c == 0 else b_scores[q], before)
                    a = adj_big[q][:, H + c * CH:H + (c + 1) * CH]
                    dve.tensor_tensor_reduce(a, score_bank[c % 3][:], a, -2.0, bound_b[:, q, 1 + c:2 + c],
                                             ALU.add, ALU.min, bound_b[:, q, 2 + c:3 + c]
                                             ).then_inc(b_scores[q], 1)

                def out_big(u, q):
                    dve.wait_ge(adj_b_free[q], u + 2)
                    dve.tensor_reduce(sum_b[:, q, 3:4], sum_b[:, q, 0:3], AX.X, ALU.add
                                      ).then_inc(b_total[q], 1)
                    dve.wait_ge(b_total[q], u + 1)
                    dve.reciprocal(sum_b[:, q, 4:5], sum_b[:, q, 3:4]).then_inc(b_recip[q], 1)
                    dve.wait_ge(b_recip[q], u + 1)
                    dve.wait_ge(b_stored[q], u * 16 + 16)
                    dve.wait_ge(b_pv[q], u * NC + NC)
                    dve.scalar_tensor_tensor(out=out_b[:, q, :], in0=out_bank[:, 0:D],
                                             scalar=sum_b[:, q, 4:5], in1=x_big[:, u * 2 + q, :],
                                             op0=ALU.mult, op1=ALU.add).then_inc(b_out[q], 1)

                def body(u, q, up, un):
                    n = u * 2 + q
                    block_cols = adj_small[q][:, bass.ds(n * P, P)]

                    def off_small(i):
                        a = adj_small[q][:, i * H:(i + 1) * H]
                        dve.tensor_scalar(a, a, OFF_SCALE, None, ALU.mult, ALU.min,
                                          accum_out=off_min[:, q, i:i + 1]).then_inc(s_off[q], 1)

                    dve.wait_ge(adj_s_in[q], u * 16 + 16)
                    dve.tensor_tensor(diag[:, q, :], block_cols, cap[:], ALU.min).then_inc(s_diag[q], 1)
                    dve.wait_ge(s_diag[q], u + 1)
                    dve.tensor_tensor(block_cols, block_cols, floor[:], ALU.max).then_inc(s_masked[q], 1)
                    dve.wait_ge(s_masked[q], u + 1)
                    off_small(0)
                    scores(u, q, 0)
                    dve.wait_ge(s_qpsum[q], u + 1)
                    dve.tensor_tensor(Qs[:, q].rearrange("p c d -> p (c d)"), m1[:, 0:KD * P],
                                      c_wide[:].rearrange("p c d -> p (c d)"), ALU.add
                                      ).then_inc(s_q[q], 1)
                    dve.wait_ge(s_vpsum[q], u + 1)
                    dve.tensor_tensor(V32[:, q, :], m0[:, 0:DU], bias_row[:], ALU.add).then_inc(s_v[q], 1)
                    off_small(1)
                    scores(u, q, 1)
                    dve.wait_ge(s_off[q], u * 2 + 2)
                    dve.scalar_tensor_tensor(out=bound_s[:, q, 0:1], in0=off_min[:, q, 0:1],
                                             scalar=off_min[:, q, 1:2], in1=V32[:, q, D:DU],
                                             op0=ALU.min, op1=ALU.add).then_inc(s_offu[q], 1)
                    tiles = fixed(dve, u + 1)
                    dve.wait_ge(const_ready, 3)
                    dve.wait_ge(s_offu[q], tiles)
                    dve.wait_ge(s_spsum[q], tiles)
                    dve.tensor_tensor_reduce(diag[:, q, :], m0[:, 0:P], diag[:, q, :], -2.0,
                                             bound_s[:, q, 0:1], ALU.add, ALU.min, bound_s[:, q, 1:2]
                                             ).then_inc(s_bound[q], 1)
                    dve.wait_ge(s_bound[q], u + 1)
                    dve.tensor_tensor(bound_s[:, q, 2:3], bound_s[:, q, 1:2], V32[:, q, D:DU],
                                      ALU.subtract).then_inc(s_stat[q], 1)
                    scores(u, q, 2)
                    scores(u, q, 3)
                    dve.wait_ge(b_scores[q], u * NC + NC)
                    dve.tensor_tensor(bound_b[:, q, 6:7], bound_b[:, q, 5:6],
                                      u_big[:, bass.ds(n, 1)], ALU.subtract).then_inc(b_stat[q], 1)
                    if up is not None:
                        out_big(up, 1 - q)
                    if un is not None:
                        off_big(un, 1 - q)
                        dve.wait_ge(x_s_in[1 - q], un * 16 + 16)
                        statistics(x_small[:, 1 - q, :], un + (NT // 2 + 1), 1 - q)
                    dve.wait_ge(adj_s_free[q], u + 2)
                    dve.tensor_tensor(sum_s[:, q, 2:3], sum_s[:, q, 0:1], sum_s[:, q, 1:2], ALU.add
                                      ).then_inc(s_total[q], 1)
                    dve.wait_ge(s_total[q], u + 1)
                    dve.reciprocal(sum_s[:, q, 3:4], sum_s[:, q, 2:3]).then_inc(s_recip[q], 1)
                    dve.wait_ge(s_recip[q], u + 1)
                    dve.wait_ge(s_stored[q], u * 16 + 16)
                    dve.wait_ge(x_s_in[q], u * 16 + 16)
                    dve.wait_ge(s_opsum[q], u + 1)
                    dve.scalar_tensor_tensor(out=out_s[:, q, :], in0=m0[:, 0:D], scalar=sum_s[:, q, 3:4],
                                             in1=x_small[:, q, :], op0=ALU.mult, op1=ALU.add
                                             ).then_inc(s_out[q], 1)
                    if un is not None:
                        normalize(x_small[:, 1 - q, :], un + (NT // 2 + 1), 1 - q)

                pairs(dve, body)
                out_big(LAST, 1)
            with dve.Else():
                dve.wait_ge(prep_done, 3)
                dve.wait_ge(g_ids, 2)
                dve.tensor_copy(g_ptr[:], ptr_row[:])
                dve.memset(g_graph[:], 0.0)
                dve.memset(g_rows[:], 0.0).then_inc(G_step, 1)
                dve.wait_ge(G_step, 2)
                with dve.Fori(0, NG) as i:
                    edge = g_ptr[:, bass.ds(i, 1)]
                    dve.scalar_tensor_tensor(out=g_graph[:], in0=g_key_id, scalar=edge, in1=g_graph[:],
                                             op0=ALU.is_ge, op1=ALU.add)
                    dve.scalar_tensor_tensor(out=g_rows[:], in0=g_row_id[:], scalar=edge,
                                             in1=g_rows[:], op0=ALU.is_ge, op1=ALU.add
                                             ).then_inc(G_step, 1)
                    dve.wait_ge(G_step, i + 3)

                with dve.Fori(0, GT) as t:
                    dve.wait_ge(x_s_in[0], t * 16 + 16)
                    statistics(x_small[:, 0, :], t + 1, 0)
                    normalize(x_small[:, 0, :], t + 1, 0)
                    dve.wait_ge(s_vpsum[0], t + 1)
                    dve.tensor_tensor(g_V[:, t, :], m1[:, 0:DU], bias_row[:], ALU.add
                                      ).then_inc(s_v[0], 1)
                dve.wait_ge(s_v[0], GT)
                dve.sem_inc(g_graphs, 1)

                with dve.Fori(0, GT) as t:
                    steps = [0]

                    def step(ins):
                        ins.then_inc(g_step, 1)
                        steps[0] += 1
                        dve.wait_ge(g_step, t * G_STEPS + steps[0])

                    dve.wait_ge(s_qpsum[0], t + 1)
                    dve.tensor_tensor(Qs[:, 0].rearrange("p c d -> p (c d)"), m1[:, 0:KD * P],
                                      c_wide[:].rearrange("p c d -> p (c d)"), ALU.add
                                      ).then_inc(s_q[0], 1)
                    step(dve.tensor_copy(g_row[:, 0:1], g_rows[:, bass.ds(t, 1)]))
                    step(dve.tensor_copy(g_row[:, 1:2], g_V[:, t, D:DU]))
                    step(dve.tensor_scalar(g_in[:], g_graph[:], g_row[:, 0:1], 2 * FARTHEST,
                                           ALU.is_equal, ALU.mult))
                    step(dve.tensor_scalar(g_in[:], g_in[:], -FARTHEST, None, ALU.add))
                    dve.wait_ge(g_adj_in, t * 16 + 16)
                    step(dve.tensor_scalar(g_z[:], g_adj[:], OFF_SCALE, g_row[:, 1:2], ALU.mult,
                                           ALU.add))
                    step(dve.scalar_tensor_tensor(out=g_z[:], in0=g_in[:], scalar=-1.0, in1=g_z[:],
                                                  op0=ALU.mult, op1=ALU.min))
                    for c in range(GC):
                        dve.wait_ge(g_spsum, t * GC + (c + 1))
                        a = g_adj[:, c * CH:(c + 1) * CH]
                        step(dve.tensor_tensor(a, score_bank[c % 2][:], a, ALU.add))
                    step(dve.scalar_tensor_tensor(out=g_adj[:], in0=g_adj[:], scalar=-2.0,
                                                  in1=g_in[:], op0=ALU.mult, op1=ALU.min))
                    step(dve.tensor_tensor(g_z[:], g_z[:], g_adj[:], ALU.max))
                    step(dve.tensor_reduce(g_row[:, 2:3], g_z[:], AX.X, ALU.min))
                    assert steps[0] == G_BOUND
                    dve.wait_ge(g_exp, t + 1)
                    step(dve.scalar_tensor_tensor(out=g_z[:], in0=g_in[:], scalar=0.0, in1=g_z[:],
                                                  op0=ALU.is_gt, op1=ALU.mult))
                    step(dve.reciprocal(g_sum[:, 1:2], g_sum[:, 0:1]))
                    dve.wait_ge(g_opsum, t + 1)
                    dve.wait_ge(g_x_in, t * 16 + 16)
                    step(dve.tensor_scalar(out_s[:, 0, :], out_bank[:, 0:D], g_sum[:, 1:2], None,
                                           ALU.mult))
                    step(dve.tensor_tensor(out_s[:, 0, :], out_s[:, 0, :], x_small[:, 1, :], ALU.add))
                    assert steps[0] == G_STEPS
                    dve.sem_inc(g_out, 1)

        @block.tensor
        def _(pe):
            pe.wait_ge(w_in, 6 * 16)
            for i in range(KD):
                for o in range(KD):
                    last = pe.matmul(m0[:, i * D:(i + 1) * D], Wq_sb[:, o, i * P:(i + 1) * P],
                                     Wk_sb[:, o, :], start=(o == 0), stop=(o == KD - 1))
            last.then_inc(prep_psum, 1)
            pe.wait_ge(ident_ready, 2)
            for i in range(KD):
                for o in range(KD):
                    last = pe.transpose(m1[:, i * D + o * P:i * D + (o + 1) * P],
                                        Wv_sb[:, o, i * P:(i + 1) * P], ident[:])
            last.then_inc(prep_psum, 1)
            pe.wait_ge(w_wide, 1)
            for k, (w, b) in enumerate(((Wk_sb, bq_col), (Wq_sb, bk_col))):
                for i in range(KD):
                    for o in range(KD):
                        pe.matmul(out_bank[:, k * KD + i:k * KD + i + 1], w[:, o, i * P:(i + 1) * P],
                                  b[:, o:o + 1], start=(o == 0), stop=(o == KD - 1))
            for o in range(KD):
                last = pe.matmul(out_bank[:, 2 * KD:2 * KD + 1], bq_wide[:, o, :], bk_col[:, o:o + 1],
                                 start=(o == 0), stop=(o == KD - 1))
            last.then_inc(prep_psum, 1)
            pe.wait_ge(prep_done, 3)

            def turn(bank, q, done):
                for c in range(KD):
                    last = pe.transpose(bank[:, c * P:(c + 1) * P], xn[:, q, c * P:(c + 1) * P],
                                        ident[:])
                last.then_inc(done[q], 1)

            def project_v(bank, q, done):
                for c in range(KD):
                    last = pe.matmul(bank[:, 0:DU], hT[:, q, c, :], WvT[:, c, :], start=(c == 0),
                                     stop=(c == KD - 1))
                last.then_inc(done[q], 1)

            with pe.If(regular_ptr(pe)):
                with pe.Fori(0, NT // 2) as u:
                    for q in range(2):
                        pe.wait_ge(p_lo[q], u + 1)
                        pe.wait_ge(xn_ready[q], u + 1)
                        turn(score_bank[q], q, p_turned)
                        pe.wait_ge(p_v32[q], u + 1)
                        pe.wait_ge(p_h32[q], u + 1)
                        project_v(turn_bank[q], q, p_vpsum)

                def q_big(u, q):
                    for j in range(KD):
                        k = 0
                        for c in range(KD):
                            for g, h in ((G_hi, hT_hi), (G_hi, hT_lo), (G_lo, hT_hi)):
                                last = pe.matmul(m1[:, j * P:(j + 1) * P], g[:, c, j * P:(j + 1) * P],
                                                 h[:, c, bass.ds((u * 2 + q) * P, P)], start=(k == 0),
                                                 stop=(k == 3 * KD - 1))
                                k += 1
                    last.then_inc(b_qpsum[q], 1)

                pe.wait_ge(G_step, 3)
                pe.wait_ge(p_lo[0], NT // 2 + 1)
                pe.wait_ge(p_lo[1], NT // 2 + 1)
                q_big(0, 0)
                pe.wait_ge(p_vlo[0], NT // 2 + 1)
                pe.wait_ge(p_vlo[1], NT // 2 + 1)

                def score_chunk(u, q, c):
                    if c == 3:
                        pe.wait_ge(b_scores[q], u * NC + 1)
                    k = 0
                    for j in range(KD):
                        for a, h in ((Qb_hi, hT_hi), (Qb_hi, hT_lo), (Qb_lo, hT_hi)):
                            last = pe.matmul(score_bank[c % 3][:], a[:, q, j, :],
                                             h[:, j, c * CH:(c + 1) * CH], start=(k == 0),
                                             stop=(k == 3 * KD - 1))
                            k += 1
                    last.then_inc(b_spsum[q], 1)

                def turn_probs(u, q, c):
                    pe.wait_ge(b_probs[q], u * 2 + (1 + c // 2))
                    if c >= 2:
                        pe.wait_ge(b_pT32[q], u * NC + (c - 1))
                    for k in range(KB):
                        last = pe.transpose(turn_bank[c % 2][:, k * P:(k + 1) * P],
                                            probs[:, (c * KB + k) * P:(c * KB + k + 1) * P], ident[:])
                    last.then_inc(b_tpsum[q], 1)

                def attend(u, q, c):
                    pe.wait_ge(b_pT[q], u * NC + (c + 1))
                    for k in range(KB):
                        b = c * KB + k
                        s = slice(k * P, (k + 1) * P)
                        for i, (a, v) in enumerate(((PT_hi, V_hi), (PT_hi, V_lo), (PT_lo, V_hi))):
                            last = pe.matmul(out_bank[:, 0:D], a[:, c, s], v[:, b, :],
                                             start=(b == 0 and i == 0), stop=(b == NT - 1 and i == 2))
                    last.then_inc(b_pv[q], 1)

                def body(u, q, up, un):
                    pe.wait_ge(xn_ready[q], u + (NT // 2 + 1))
                    if up is not None:
                        pe.wait_ge(s_out[1 - q], up + 2)
                    turn(m0, q, s_turned)
                    pe.wait_ge(b_q[q], u + 1)
                    if up is not None:
                        pe.wait_ge(b_scores[1 - q], up * NC + NC)
                    score_chunk(u, q, 0)
                    pe.wait_ge(s_hT[q], u + 1)
                    pe.wait_ge(b_q32[q], u + 1)
                    for j in range(KD):
                        for c in range(KD):
                            last = pe.matmul(m1[:, j * P:(j + 1) * P], G32[:, c, j * P:(j + 1) * P],
                                             hT[:, q, c, :], start=(c == 0), stop=(c == KD - 1))
                    last.then_inc(s_qpsum[q], 1)
                    project_v(m0, q, s_vpsum)
                    score_chunk(u, q, 1)
                    pe.wait_ge(s_q[q], u + 1)
                    pe.wait_ge(s_v[q], u + 1)
                    for c in range(KD):
                        last = pe.matmul(m0[:, 0:P], Qs[:, q, c, :], hT[:, q, c, :], start=(c == 0),
                                         stop=(c == KD - 1))
                    last.then_inc(s_spsum[q], 1)
                    score_chunk(u, q, 2)
                    if up is not None:
                        attend(up, 1 - q, 0)
                    score_chunk(u, q, 3)
                    if up is not None:
                        attend(up, 1 - q, 1)
                    pe.wait_ge(s_probs[q], u + 1)
                    pe.transpose(m1[:, 0:P], diag[:, q, :], ident[:]).then_inc(s_tpsum[q], 1)
                    if up is not None:
                        attend(up, 1 - q, 2)
                        attend(up, 1 - q, 3)
                    pe.wait_ge(s_pT[q], u + 1)
                    pe.wait_ge(s_stat[q], u + 1)
                    pe.matmul(m0[:, 0:D], PsT[:, q, :], V32[:, q, 0:D], start=True, stop=True
                              ).then_inc(s_opsum[q], 1)
                    for c in range(NC):
                        turn_probs(u, q, c)
                    if un is not None:
                        q_big(un, 1 - q)
                    if up is not None:
                        pe.wait_ge(b_out[1 - q], up + 1)

                pairs(pe, body)
                for c in range(NC):
                    attend(LAST, 1, c)
            with pe.Else():
                with pe.Fori(0, GT) as t:
                    pe.wait_ge(xn_ready[0], t + 1)
                    turn(m0, 0, s_turned)
                    pe.wait_ge(s_hT[0], t + 1)
                    project_v(m1, 0, s_vpsum)
                    pe.wait_ge(s_v[0], t + 1)
                with pe.Fori(0, GT) as t:
                    for j in range(KD):
                        for c in range(KD):
                            last = pe.matmul(m1[:, j * P:(j + 1) * P], G32[:, c, j * P:(j + 1) * P],
                                             g_hT[:, c, bass.ds(t * P, P)], start=(c == 0),
                                             stop=(c == KD - 1))
                    last.then_inc(s_qpsum[0], 1)
                    pe.wait_ge(s_q[0], t + 1)
                    for c in range(GC):
                        if c >= 2:
                            pe.wait_ge(g_step, t * G_STEPS + (5 + c))
                        for j in range(KD):
                            last = pe.matmul(score_bank[c % 2][:], Qs[:, 0, j, :],
                                             g_hT[:, j, c * CH:(c + 1) * CH], start=(j == 0),
                                             stop=(j == KD - 1))
                        last.then_inc(g_spsum, 1)
                    pe.wait_ge(g_step, t * G_STEPS + (G_BOUND + 1))
                    for c in range(GC):
                        if c >= 2:
                            pe.wait_ge(g_turned, t * GC + (c - 1))
                        for k in range(KB):
                            b = c * KB + k
                            last = pe.transpose(turn_bank[c % 2][:, k * P:(k + 1) * P],
                                                g_z[:, b * P:(b + 1) * P], ident[:])
                        last.then_inc(g_tpsum, 1)
                    pe.wait_ge(g_turned, t * GC + GC)
                    for b in range(GT):
                        last = pe.matmul(out_bank[:, 0:D], g_adj[:, b * P:(b + 1) * P],
                                         g_V[:, b, 0:D], start=(b == 0), stop=(b == GT - 1))
                    last.then_inc(g_opsum, 1)
                    pe.wait_ge(g_out, t + 1)


_INS = ['x', 'adj', 'L0_gnn_ptr', 'L0_gnn_Wq', 'L0_gnn_bq', 'L0_gnn_Wk', 'L0_gnn_bk', 'L0_gnn_Wv', 'L0_gnn_bv']


def kernel(**inputs):
    import numpy as _np
    import concourse.bacc as _bacc
    from concourse import mybir as _mybir
    from concourse.bass_utils import run_bass_kernel_spmd as _run

    nc = _bacc.Bacc("TRN2", target_bir_lowering=False, num_devices=1)
    arrays, args = {}, []
    for name in _INS:
        a = _np.ascontiguousarray(inputs[name])
        arrays[f"in_{name}"] = a
        args.append(nc.dram_tensor(f"in_{name}", a.shape, _mybir.dt.from_np(a.dtype), kind="ExternalInput").ap())
    shape = inputs['x'].shape
    args.append(nc.dram_tensor("out_0", shape, _mybir.dt.float32, kind="ExternalOutput").ap())
    build_program(nc, *args)
    r = _run(nc, [arrays], core_ids=[0])
    return r.results[0]["out_0"]
```

```python
from contextlib import ExitStack

import concourse.bass as bass
from concourse import mybir

P = 128
BIG = 3.0e38
FAR = 1.0e30
FARTHEST = 1.5e38
OFF_SCALE = 2.0e6
EPS = 1e-5

ALU = mybir.AluOpType
ACT = mybir.ActivationFunctionType
AX = mybir.AxisListType
F32 = mybir.dt.float32
F32R = mybir.dt.float32r
I32 = mybir.dt.int32


def build_program(nc, x, adj, ptr, Wq, bq, Wk, bk, Wv, bv, out):
    N, D = x.shape
    H = N // 2
    NT = H // P
    NG = ptr.shape[0]
    GS = H // (ptr.shape[0] - 1)
    KD = D // P
    CH = 512
    NC = H // CH
    KB = CH // P
    GT = N // P
    GC = N // CH
    DU = D + 1
    SC = 1.0 / float(D) ** 0.5

    with ExitStack() as ctx:
        def sb(name, shape, dt=F32, to=ctx):
            return to.enter_context(nc.sbuf_tensor(name, shape, dt))

        def ps(name):
            return ctx.enter_context(nc.psum_tensor(name, [P, 512], F32))

        def sem(name):
            return ctx.enter_context(nc.semaphore(name))

        def sem2(name):
            return [sem(name + "0"), sem(name + "1")]

        score_bank = [ps(f"score_bank{i}") for i in range(3)]
        turn_bank = [ps(f"turn_bank{i}") for i in range(2)]
        out_bank = ps("out_bank")
        m0 = ps("m0")
        m1 = ps("m1")

        x_big = sb("x_big", [P, NT + 1, D])
        x_small = sb("x_small", [P, 2, D])
        probs = sb("probs", [P, H])
        G32 = sb("G32", [P, KD, D])
        WvT = sb("WvT", [P, KD, DU])
        bias_row = sb("bias_row", [P, DU])
        c_col = sb("c_col", [P, KD])
        c_wide = sb("c_wide", [P, KD, P])
        ident = sb("ident", [P, P])
        cap = sb("cap", [P, P])
        floor = sb("floor", [P, P])
        bq_col = sb("bq_col", [P, KD])
        bk_col = sb("bk_col", [P, KD])
        half = sb("half", [P, 1])
        W_sb = probs[:, 0:3 * KD * D].rearrange("p (w c d) -> p w c d", w=3, c=KD)
        Wq_sb, Wk_sb, Wv_sb = W_sb[:, 0], W_sb[:, 1], W_sb[:, 2]
        bq_wide = probs[:, 3 * KD * D:3 * KD * D + KD * P].rearrange("p (c d) -> p c d", c=KD)
        all_moments = sb("all_moments", [P, NT + 1, 6])
        all_mean_var = sb("all_mean_var", [P, NT + 1, 2])
        all_var_eps = sb("all_var_eps", [P, NT + 1])
        all_rstd = sb("all_rstd", [P, NT + 1])
        ptr_row = sb("ptr_row", [P, NG], I32)
        ptr_drawn = sb("ptr_drawn", [P, NG], I32)
        ptr_same = sb("ptr_same", [P, NG])
        path = sb("path", [P, 1], I32)
        moments = sb("moments", [P, 2, 6])
        mean_var = sb("mean_var", [P, 2, 2])
        var_eps = sb("var_eps", [P, 2])
        rstd = sb("rstd", [P, 2])
        xn = sb("xn", [P, 2, D])
        hT = sb("hT", [P, 2, KD, P])
        V32 = sb("V32", [P, 2, DU])
        Qs = sb("Qs", [P, 2, KD, P])
        out_s = sb("out_s", [P, 2, D])

        with ExitStack() as regular:
            adj_big = [sb(f"adj_big{i}", [P, N], to=regular) for i in range(2)]
            adj_small = [sb(f"adj_small{i}", [P, N], to=regular) for i in range(2)]
            hT_hi = sb("hT_hi", [P, KD, H], F32R, to=regular)
            hT_lo = sb("hT_lo", [P, KD, H], F32R, to=regular)
            V_hi = sb("V_hi", [P, NT, D], F32R, to=regular)
            V_lo = sb("V_lo", [P, NT, D], F32R, to=regular)
            u_big = sb("u_big", [P, NT], to=regular)
            PT32 = sb("PT32", [P, 2, CH], to=regular)
            PT_hi = sb("PT_hi", [P, NC, CH], F32R, to=regular)
            PT_lo = sb("PT_lo", [P, NC, CH], F32R, to=regular)
            G_hi = sb("G_hi", [P, KD, D], F32R, to=regular)
            G_lo = sb("G_lo", [P, KD, D], F32R, to=regular)
            Qb32 = sb("Qb32", [P, KD, P], to=regular)
            Qb_hi = sb("Qb_hi", [P, 2, KD, P], F32R, to=regular)
            Qb_lo = sb("Qb_lo", [P, 2, KD, P], F32R, to=regular)
            diag = sb("diag", [P, 2, P], to=regular)
            PsT = sb("PsT", [P, 2, P], to=regular)
            off_min = sb("off_min", [P, 2, 2], to=regular)
            bound_s = sb("bound_s", [P, 2, 3], to=regular)
            bound_b = sb("bound_b", [P, 2, 7], to=regular)
            sum_s = sb("sum_s", [P, 2, 5], to=regular)
            sum_b = sb("sum_b", [P, 2, 5], to=regular)
            out_b = sb("out_b", [P, 2, D], to=regular)
            xn_two = [xn[:], PT32[:, 0, :].rearrange("p (i d) -> p i d", i=2)]
            hT_two = [hT[:].rearrange("p a b q -> p (a b q)"), out_b[:].rearrange("p i d -> p (i d)")]
            V_two = [V32[:], probs[:, 0:2 * DU].rearrange("p (i d) -> p i d", i=2)]
            V_two_bank = [turn_bank, [out_bank, score_bank[2]]]

        with ExitStack() as general:
            g_hT = sb("g_hT", [P, KD, N], to=general)
            g_V = sb("g_V", [P, N // P, DU], to=general)
            g_graph = sb("g_graph", [P, N], to=general)
            g_adj = sb("g_adj", [P, N], to=general)
            g_in = sb("g_in", [P, N], to=general)
            g_z = sb("g_z", [P, N], to=general)
            g_rows = sb("g_rows", [P, N // P], to=general)
            g_row_id = sb("g_row_id", [P, N // P], I32, to=general)
            g_ptr = sb("g_ptr", [P, NG], to=general)
            g_row = sb("g_row", [P, 3], to=general)
            g_sum = sb("g_sum", [P, GC + 2], to=general)
            g_key_id = g_z[:].bitcast(I32)

        w_in = sem("w_in")
        x_in = [sem(f"x_in{i}") for i in range(5)]
        ptr_in = sem("ptr_in")
        ptr_id = sem("ptr_id")
        ptr_step = sem("ptr_step")
        path_known = sem("path_known")
        w_wide = sem("w_wide")
        const_ready = sem("const_ready")
        ident_ready = sem("ident_ready")
        prep_psum = sem("prep_psum")
        prep_done = sem("prep_done")
        c_done = sem("c_done")
        c_spread = sem("c_spread")
        G_psum = sem("G_psum")
        G_step = sem("G_step")
        g_clear = sem("g_clear")
        moments_done = sem2("moments_done")
        mean_done = sem2("mean_done")
        var_ready = sem2("var_ready")
        rstd_ready = sem2("rstd_ready")
        xn_ready = sem2("xn_ready")
        p_moments = sem("p_moments")
        p_mean = sem("p_mean")
        p_var = sem("p_var")
        p_rstd = sem("p_rstd")
        p_xn = sem2("p_xn")
        p_turned = sem2("p_turned")
        p_h32 = sem2("p_h32")
        p_hi = sem2("p_hi")
        p_lo = sem2("p_lo")
        p_vpsum = sem2("p_vpsum")
        p_v32 = sem2("p_v32")
        p_vhi = sem2("p_vhi")
        p_vlo = sem2("p_vlo")
        adj_b_in = sem2("adj_b_in")
        adj_s_in = sem2("adj_s_in")
        x_s_in = sem2("x_s_in")
        adj_b_free = sem2("adj_b_free")
        adj_s_free = sem2("adj_s_free")
        s_turned = sem2("s_turned")
        s_hT = sem2("s_hT")
        s_qpsum = sem2("s_qpsum")
        s_vpsum = sem2("s_vpsum")
        s_q = sem2("s_q")
        s_v = sem2("s_v")
        s_spsum = sem2("s_spsum")
        s_diag = sem2("s_diag")
        s_masked = sem2("s_masked")
        s_off = sem2("s_off")
        s_offu = sem2("s_offu")
        s_bound = sem2("s_bound")
        s_stat = sem2("s_stat")
        s_probs = sem2("s_probs")
        s_outside = sem2("s_outside")
        s_tpsum = sem2("s_tpsum")
        s_pT = sem2("s_pT")
        s_opsum = sem2("s_opsum")
        s_total = sem2("s_total")
        s_recip = sem2("s_recip")
        s_out = sem2("s_out")
        s_stored = sem2("s_stored")
        b_qpsum = sem2("b_qpsum")
        b_q32 = sem2("b_q32")
        b_qhi = sem2("b_qhi")
        b_q = sem2("b_q")
        b_off = sem2("b_off")
        b_offu = sem2("b_offu")
        b_spsum = sem2("b_spsum")
        b_scores = sem2("b_scores")
        b_stat = sem2("b_stat")
        b_probs = sem2("b_probs")
        b_tpsum = sem2("b_tpsum")
        b_pT32 = sem2("b_pT32")
        b_pT = sem2("b_pT")
        b_pv = sem2("b_pv")
        b_total = sem2("b_total")
        b_recip = sem2("b_recip")
        b_out = sem2("b_out")
        b_stored = sem2("b_stored")

        g_ids = sem("g_ids")
        g_graphs = sem("g_graphs")
        g_adj_in = sem("g_adj_in")
        g_step = sem("g_step")
        g_exp = sem("g_exp")
        g_spsum = sem("g_spsum")
        g_tpsum = sem("g_tpsum")
        g_turned = sem("g_turned")
        g_opsum = sem("g_opsum")
        g_out = sem("g_out")
        g_stored = sem("g_stored")
        g_x_in = sem("g_x_in")

        LAST = NT // 2 - 1
        Q4 = NT // 4
        LOTS = [(i * Q4, (i + 1) * Q4) for i in range(4)] + [(NT, NT + 1)]
        G_BOUND = GC + 9
        G_STEPS = G_BOUND + 5

        def regular_ptr(eng):
            eng.wait_ge(path_known, 1)
            return eng.value_load(path[0:1, 0:1], min_val=0, max_val=1) == 1

        def fixed(eng, value):
            return value if isinstance(value, int) else eng.to_reg(value)

        def alternate(eng, count, body):
            last = count // 2 - 1
            body(0, 0, None, 0)
            with eng.Fori(0, last) as it:
                body(it, 1, it, it + 1)
                body(it + 1, 0, it, it + 1)
            body(last, 1, last, None)

        block = ctx.enter_context(nc.Block())

        @block.sync
        def _(sp):
            sp.dma_start(ptr_row[:], ptr.rearrange("(a d) -> a d", a=1).broadcast_to([P, NG])
                         ).then_inc(ptr_in, 16)
            for w, dst in ((Wq, Wq_sb), (Wk, Wk_sb), (Wv, Wv_sb)):
                sp.dma_start(dst, w.rearrange("(c p) d -> p c d", p=P)).then_inc(w_in, 16)
            sp.dma_start(bq_col[:], bq.rearrange("(c p) -> p c", p=P),
                         allow_slow_non_contiguous=True).then_inc(w_in, 16)
            sp.dma_start(bk_col[:], bk.rearrange("(c p) -> p c", p=P),
                         allow_slow_non_contiguous=True).then_inc(w_in, 16)
            sp.dma_start(bias_row[:, 0:D], bv.rearrange("(a d) -> a d", a=1).broadcast_to([P, D])
                         ).then_inc(w_in, 16)
            for i, (a, b) in enumerate(LOTS):
                rows = x[H + a * P:H + b * P, :] if a < NT else x[0:P, :]
                sp.dma_start(x_big[:, a:b, :], rows.rearrange("(t p) d -> p t d", p=P)
                             ).then_inc(x_in[i], 16)

            with sp.If(regular_ptr(sp)):
                def load(u, q):
                    n = u * 2 + q
                    sp.wait_ge(adj_s_free[q], u + 1)
                    sp.dma_start(adj_small[q][:], adj[bass.ds(n * P, P), :]).then_inc(adj_s_in[q], 16)
                    sp.wait_ge(s_out[q], u + 1)
                    sp.dma_start(x_small[:, q, :], x[bass.ds(n * P, P), :]).then_inc(x_s_in[q], 16)
                    sp.wait_ge(adj_b_free[q], u + 1)
                    sp.dma_start(adj_big[q][:], adj[bass.ds(n * P + H, P), :]).then_inc(adj_b_in[q], 16)

                with sp.Fori(0, NT // 2) as u:
                    load(u, 0)
                    load(u, 1)
            with sp.Else():
                def g_rows_of(a, t):
                    return a[bass.ds(t * P, P), :]

                sp.dma_start(x_small[:, 0, :], g_rows_of(x, 0)).then_inc(x_s_in[0], 16)
                with sp.Fori(1, GT) as t:
                    sp.wait_ge(xn_ready[0], t)
                    sp.dma_start(x_small[:, 0, :], g_rows_of(x, t)).then_inc(x_s_in[0], 16)
                sp.wait_ge(g_graphs, 1)
                sp.dma_start(g_adj[:], g_rows_of(adj, 0)).then_inc(g_adj_in, 16)
                sp.dma_start(x_small[:, 1, :], g_rows_of(x, 0)).then_inc(g_x_in, 16)
                with sp.Fori(1, GT) as t:
                    sp.wait_ge(g_out, t)
                    sp.dma_start(g_rows_of(out, t - 1), out_s[:, 0, :]).then_inc(g_stored, 16)
                    sp.wait_ge(g_stored, t * 16)
                    sp.dma_start(g_adj[:], g_rows_of(adj, t)).then_inc(g_adj_in, 16)
                    sp.dma_start(x_small[:, 1, :], g_rows_of(x, t)).then_inc(g_x_in, 16)
                sp.wait_ge(g_out, GT)
                sp.dma_start(g_rows_of(out, GT - 1), out_s[:, 0, :]).then_inc(g_stored, 16)
                sp.wait_ge(g_stored, GT * 16)

        @block.scalar
        def _(act):
            for q in range(2):
                act.sem_inc(adj_s_free[q], 1)
                act.sem_inc(adj_b_free[q], 1)
            act.wait_ge(prep_psum, 1)
            act.activation(WvT[:, :, 0:D], m1[:, 0:KD * D].rearrange("p (c d) -> p c d", c=KD),
                           ACT.Copy).then_inc(prep_done, 1)
            act.wait_ge(G_psum, 1)
            act.activation(G32[:].rearrange("p c d -> p (c d)"), m0[:, 0:KD * D], ACT.Copy,
                           scale=SC / 2).then_inc(G_step, 1)

            with act.If(regular_ptr(act)):
                def turn_in(u, q):
                    act.wait_ge(p_turned[q], u + 1)
                    src = score_bank[q][:]
                    act.activation(hT_two[q], src, ACT.Relu).then_inc(p_h32[q], 1)
                    act.activation(hT_hi[:, :, bass.ds((u * 2 + q) * 2 * P, 2 * P)],
                                   src.rearrange("p (c d) -> p c d", c=KD), ACT.Relu
                                   ).then_inc(p_hi[q], 1)

                def before(u, q, up, un):
                    if un is not None:
                        turn_in(un, 1 - q)
                    tiles = fixed(act, u + 2)
                    act.wait_ge(prep_done, 2)
                    act.wait_ge(p_v32[q], tiles)
                    act.activation(V_hi[:, bass.ds((u * 2 + q) * 2, 2), :], V_two[q][:, :, 0:D],
                                   ACT.Copy).then_inc(p_vhi[q], 1)

                turn_in(0, 0)
                alternate(act, NT // 2, before)

                def q_big(u, q):
                    act.wait_ge(b_qpsum[q], u + 1)
                    for c in range(KD):
                        last = act.activation(Qb32[:, c, :], m1[:, c * P:(c + 1) * P], ACT.Identity,
                                              bias=c_col[:, c:c + 1])
                    last.then_inc(b_q32[q], 1)

                q_big(0, 0)

                def turn_in_small(u, q):
                    act.wait_ge(s_turned[q], u + 1)
                    act.activation(hT[:, q].rearrange("p c d -> p (c d)"), m1[:, 0:D], ACT.Relu
                                   ).then_inc(s_hT[q], 1)

                turn_in_small(0, 0)

                def off_small(q, i):
                    a = adj_small[q][:, i * H:(i + 1) * H]
                    act.activation(a, a, ACT.Exp, bias=bound_s[:, q, 2:3], scale=-1.0,
                                   accum_out=sum_s[:, q, 1 + i:2 + i]
                                   ).then_inc(s_outside[q] if i == 0 else adj_s_free[q], 1)

                def exp_big(q, i):
                    act.activation(probs[:, i * H // 2:(i + 1) * H // 2],
                                   adj_big[q][:, H + i * H // 2:H + (i + 1) * H // 2], ACT.Exp,
                                   bias=bound_b[:, q, 5:6], scale=-1.0,
                                   accum_out=sum_b[:, q, i:i + 1]).then_inc(b_probs[q], 1)

                def body(u, q, up, un):
                    act.wait_ge(s_stat[q], u + 1)
                    act.activation(diag[:, q, :], diag[:, q, :], ACT.Exp, bias=bound_s[:, q, 1:2],
                                   scale=-1.0, accum_out=sum_s[:, q, 0:1]).then_inc(s_probs[q], 1)
                    if un is not None:
                        q_big(un, 1 - q)
                    off_small(q, 0)
                    act.wait_ge(s_tpsum[q], u + 1)
                    act.copy(PsT[:, q, :], m1[:, 0:P]).then_inc(s_pT[q], 1)
                    act.wait_ge(b_stat[q], u + 1)
                    exp_big(q, 0)
                    off_small(q, 1)
                    exp_big(q, 1)
                    if un is not None:
                        turn_in_small(un, 1 - q)
                    for c in range(NC):
                        act.wait_ge(b_tpsum[q], u * NC + (c + 1))
                        if up is not None:
                            act.wait_ge(b_pv[1 - q], up * NC + (c + 1))
                        act.copy(PT_hi[:, c, :], turn_bank[c % 2][:])
                        if c >= 2:
                            act.wait_ge(b_pT[q], u * NC + (c - 1))
                        elif up is not None:
                            act.wait_ge(b_pT[1 - q], up * NC + (c + 3))
                        act.copy(PT32[:, c % 2, :], turn_bank[c % 2][:]).then_inc(b_pT32[q], 1)
                    act.activation(adj_big[q][:, 0:H], adj_big[q][:, 0:H], ACT.Exp,
                                   bias=bound_b[:, q, 6:7], scale=-1.0,
                                   accum_out=sum_b[:, q, 2:3]).then_inc(adj_b_free[q], 1)
                    if up is not None:
                        store(up, 1 - q)

                def store(u, q):
                    act.wait_ge(s_out[q], u + 2)
                    act.dma_start(out[bass.ds((u * 2 + q) * P, P), :], out_s[:, q, :]
                                  ).then_inc(s_stored[q], 16)
                    act.wait_ge(b_out[q], u + 2)
                    act.dma_start(out[bass.ds((u * 2 + q) * P + H, P), :], out_b[:, q, :]
                                  ).then_inc(b_stored[q], 16)

                alternate(act, NT, body)
                store(LAST, 1)
                for q in range(2):
                    act.wait_ge(s_stored[q], 16 * (NT // 2 + 1))
                    act.wait_ge(b_stored[q], 16 * (NT // 2 + 1))
            with act.Else():
                with act.Fori(0, GT) as t:
                    act.wait_ge(s_turned[0], t + 1)
                    act.activation(hT[:, 0].rearrange("p c d -> p (c d)"), m0[:, 0:D], ACT.Relu)
                    act.activation(g_hT[:, :, bass.ds(t * P, P)],
                                   m0[:, 0:D].rearrange("p (c d) -> p c d", c=KD), ACT.Relu
                                   ).then_inc(s_hT[0], 1)
                with act.Fori(0, GT) as t:
                    act.wait_ge(g_step, t * G_STEPS + G_BOUND)
                    for c in range(GC):
                        a = g_z[:, c * CH:(c + 1) * CH]
                        last = act.activation(a, a, ACT.Exp, bias=g_row[:, 2:3], scale=-1.0,
                                              accum_out=g_sum[:, c:c + 1])
                    last.then_inc(g_exp, 1)
                    for c in range(GC):
                        act.wait_ge(g_tpsum, t * GC + (c + 1))
                        act.copy(g_adj[:, c * CH:(c + 1) * CH], turn_bank[c % 2][:]
                                 ).then_inc(g_turned, 1)

        @block.gpsimd
        def _(pool):
            for q in range(2):
                pool.sem_inc(p_vlo[q], 1)
            pool.memset(ident[:], 0.0).then_inc(ident_ready, 1)
            pool.wait_ge(ident_ready, 1)
            pool.affine_select(out=ident[:], in_=ident[:], compare_op=ALU.not_equal, fill=1.0, base=0,
                               pattern=[[-1, P]], channel_multiplier=1).then_inc(ident_ready, 1)
            pool.memset(half[:], -0.5).then_inc(ident_ready, 1)
            pool.wait_ge(ident_ready, 3)
            pool.iota(ptr_drawn[:], pattern=[[GS, NG]], base=0, channel_multiplier=0
                      ).then_inc(ptr_id, 1)

            def root(count, q):
                pool.wait_ge(var_ready[q], count)
                pool.tensor_tensor(rstd[:, q:q + 1], var_eps[:, q:q + 1], half[:, 0:1], ALU.pow
                                   ).then_inc(rstd_ready[q], 1)

            with pool.If(regular_ptr(pool)):
                for i, (a, b) in enumerate(LOTS):
                    pool.wait_ge(p_var, i + 1)
                    pool.tensor_tensor(all_rstd[:, a:b], all_var_eps[:, a:b],
                                       half[:, 0:1].broadcast_to([P, b - a]), ALU.pow
                                       ).then_inc(p_rstd, 1)

                def before(u, q, up, un):
                    at = bass.ds((u * 2 + q) * 2, 2)
                    pool.wait_ge(p_vhi[q], u + 1)
                    pool.tensor_tensor(V_lo[:, at, :], V_two[q][:, :, 0:D],
                                       V_hi[:, at, :].bitcast(F32), ALU.subtract)
                    pool.tensor_copy(u_big[:, at], V_two[q][:, :, D]).then_inc(p_vlo[q], 1)

                alternate(pool, NT // 2, before)

                def q_split(u, q):
                    tiles = fixed(pool, u + 1)
                    pool.wait_ge(ident_ready, 3)
                    pool.wait_ge(b_q32[q], tiles)
                    pool.tensor_scalar(Qb_hi[:, q], Qb32[:], 1.0, 0.0, ALU.mult, ALU.add
                                       ).then_inc(b_qhi[q], 1)
                    pool.wait_ge(b_qhi[q], u + 1)
                    pool.tensor_tensor(Qb_lo[:, q], Qb32[:], Qb_hi[:, q].bitcast(F32), ALU.subtract
                                       ).then_inc(b_q[q], 1)

                q_split(0, 0)

                def body(u, q, up, un):
                    if un is not None:
                        root(un + (1 - q), 1 - q)
                        q_split(un, 1 - q)
                    for c in range(NC):
                        pool.wait_ge(b_pT32[q], u * NC + (c + 1))
                        pool.tensor_tensor(PT_lo[:, c, :], PT32[:, c % 2, :], PT_hi[:, c, :].bitcast(F32),
                                           ALU.subtract).then_inc(b_pT[q], 1)

                alternate(pool, NT, body)
            with pool.Else():
                pool.iota(g_key_id, pattern=[[1, N]], base=0, channel_multiplier=0).then_inc(g_ids, 1)
                pool.iota(g_row_id[:], pattern=[[P, GT]], base=0, channel_multiplier=1
                          ).then_inc(g_ids, 1)
                with pool.Fori(0, GT) as t:
                    root(t + 1, 0)

        @block.vector
        def _(dve):
            for q in range(2):
                dve.sem_inc(p_lo[q], 1)
                dve.sem_inc(p_v32[q], 1)
                dve.sem_inc(s_out[q], 1)
                dve.sem_inc(b_out[q], 1)
                dve.sem_inc(s_stored[q], 16)
                dve.sem_inc(b_stored[q], 16)
            dve.wait_ge(ptr_in, 16)
            dve.wait_ge(ptr_id, 1)
            dve.tensor_tensor(ptr_same[:], ptr_row[:], ptr_drawn[:], ALU.is_equal).then_inc(ptr_step, 1)
            dve.wait_ge(ptr_step, 1)
            dve.tensor_reduce(path[:], ptr_same[:], AX.X, ALU.min).then_inc(path_known, 1)
            dve.memset(cap[:], -FAR).then_inc(const_ready, 1)
            dve.memset(floor[:], -BIG).then_inc(const_ready, 1)
            dve.wait_ge(const_ready, 2)
            for g in range(P // GS):
                s = slice(g * GS, (g + 1) * GS)
                dve.memset(cap[s, s], BIG)
                last = dve.memset(floor[s, s], FAR)
            last.then_inc(const_ready, 1)
            dve.wait_ge(const_ready, 3)
            dve.wait_ge(w_in, 6 * 16)
            for c in range(KD):
                last = dve.tensor_scalar(bq_wide[:, c, :], cap[:], 0.0, bq_col[:, c:c + 1], ALU.mult,
                                         ALU.add)
            last.then_inc(w_wide, 1)
            for i, (a, b) in enumerate(LOTS):
                dve.wait_ge(x_in[i], 16)
                for t in range(a, b):
                    last = dve.bn_stats(all_moments[:, t, :], x_big[:, t, :])
                last.then_inc(p_moments, 1)
                dve.wait_ge(p_moments, i + 1)
                for t in range(a, b):
                    last = dve.bn_aggr(all_mean_var[:, t, :], all_moments[:, t, :])
                last.then_inc(p_mean, 1)
                dve.wait_ge(p_mean, i + 1)
                dve.tensor_scalar(all_var_eps[:, a:b], all_mean_var[:, a:b, 1], EPS, None, ALU.add
                                  ).then_inc(p_var, 1)
            dve.wait_ge(prep_psum, 2)
            dve.tensor_scalar(c_col[:], out_bank[:, 0:KD], SC / 2, None, ALU.mult).then_inc(c_done, 1)
            dve.tensor_scalar(WvT[:, :, D], out_bank[:, KD:2 * KD], SC, None, ALU.mult)
            dve.tensor_scalar(bias_row[:, D:DU], out_bank[:, 2 * KD:2 * KD + 1], SC, None, ALU.mult
                              ).then_inc(prep_done, 1)
            dve.wait_ge(c_done, 1)
            for c in range(KD):
                last = dve.tensor_scalar(c_wide[:, c, :], cap[:], 0.0, c_col[:, c:c + 1], ALU.mult,
                                         ALU.add)
            last.then_inc(c_spread, 1)
            dve.wait_ge(c_spread, 1)

            def statistics(src, count, q):
                dve.bn_stats(moments[:, q, :], src).then_inc(moments_done[q], 1)
                count = fixed(dve, count)
                dve.wait_ge(const_ready, 3)
                dve.wait_ge(moments_done[q], count)
                dve.bn_aggr(mean_var[:, q, :], moments[:, q, :]).then_inc(mean_done[q], 1)
                dve.wait_ge(mean_done[q], count)
                dve.tensor_scalar(var_eps[:, q:q + 1], mean_var[:, q, 1:2], EPS, None, ALU.add
                                  ).then_inc(var_ready[q], 1)

            def normalize(src, count, q):
                dve.wait_ge(rstd_ready[q], count)
                dve.tensor_scalar(xn[:, q, :], src, mean_var[:, q, 0:1], rstd[:, q:q + 1],
                                  ALU.subtract, ALU.mult).then_inc(xn_ready[q], 1)

            with dve.If(regular_ptr(dve)):
                def normalize_big(u, q):
                    for i in range(2):
                        n = (u * 2 + q) * 2 + i
                        last = dve.tensor_scalar(xn_two[q][:, i, :], x_big[:, n, :],
                                                 all_mean_var[:, n, 0:1], all_rstd[:, bass.ds(n, 1)],
                                                 ALU.subtract, ALU.mult)
                    last.then_inc(p_xn[q], 1)

                dve.wait_ge(p_rstd, len(LOTS))
                normalize_big(0, 0)
                dve.wait_ge(G_step, 1)
                dve.tensor_copy(G_hi[:], G32[:]).then_inc(G_step, 1)
                dve.wait_ge(G_step, 2)
                dve.tensor_tensor(G_lo[:], G32[:], G_hi[:].bitcast(F32), ALU.subtract
                                  ).then_inc(G_step, 1)

                def before(u, q, up, un):
                    if un is not None:
                        normalize_big(un, 1 - q)
                    dve.wait_ge(p_hi[q], u + 1)
                    at = bass.ds((u * 2 + q) * 2 * P, 2 * P)
                    dve.scalar_tensor_tensor(out=hT_lo[:, :, at],
                                             in0=score_bank[q][:].rearrange("p (c d) -> p c d", c=KD),
                                             scalar=0.0, in1=hT_hi[:, :, at].bitcast(F32),
                                             op0=ALU.max, op1=ALU.subtract).then_inc(p_lo[q], 1)
                    dve.wait_ge(p_vlo[q], u + 1)
                    dve.wait_ge(p_vpsum[q], u + 1)
                    for i in range(2):
                        last = dve.tensor_tensor(V_two[q][:, i, :], V_two_bank[q][i][:, 0:DU],
                                                 bias_row[:], ALU.add)
                    last.then_inc(p_v32[q], 1)

                alternate(dve, NT // 2, before)
                dve.tensor_scalar(xn[:, 0, :], x_big[:, NT, :], all_mean_var[:, NT, 0:1],
                                  all_rstd[:, NT:NT + 1], ALU.subtract, ALU.mult
                                  ).then_inc(xn_ready[0], 1)

                def off_big(u, q):
                    dve.wait_ge(adj_b_in[q], u * 16 + 16)
                    dve.tensor_scalar(adj_big[q][:, 0:H], adj_big[q][:, 0:H], OFF_SCALE, None, ALU.mult,
                                      ALU.min, accum_out=bound_b[:, q, 0:1]).then_inc(b_off[q], 1)
                    dve.wait_ge(b_off[q], u + 1)
                    dve.tensor_tensor(bound_b[:, q, 1:2], bound_b[:, q, 0:1],
                                      u_big[:, bass.ds(u * 2 + q, 1)], ALU.add).then_inc(b_offu[q], 1)

                dve.wait_ge(p_vlo[1], NT // 4 + 1)
                off_big(0, 0)

                def scores(u, q, c):
                    products = fixed(dve, u * NC + (c + 1))
                    before = fixed(dve, u + 1 if c == 0 else u * NC + c)
                    dve.wait_ge(const_ready, 3)
                    dve.wait_ge(b_spsum[q], products)
                    dve.wait_ge(b_offu[q] if c == 0 else b_scores[q], before)
                    a = adj_big[q][:, H + c * CH:H + (c + 1) * CH]
                    dve.tensor_tensor_reduce(a, score_bank[c % 3][:], a, -2.0, bound_b[:, q, 1 + c:2 + c],
                                             ALU.add, ALU.min, bound_b[:, q, 2 + c:3 + c]
                                             ).then_inc(b_scores[q], 1)

                def out_big(u, q):
                    dve.wait_ge(adj_b_free[q], u + 2)
                    dve.tensor_reduce(sum_b[:, q, 3:4], sum_b[:, q, 0:3], AX.X, ALU.add
                                      ).then_inc(b_total[q], 1)
                    dve.wait_ge(b_total[q], u + 1)
                    dve.reciprocal(sum_b[:, q, 4:5], sum_b[:, q, 3:4]).then_inc(b_recip[q], 1)
                    dve.wait_ge(b_recip[q], u + 1)
                    dve.wait_ge(b_stored[q], u * 16 + 16)
                    dve.wait_ge(b_pv[q], u * NC + NC)
                    dve.scalar_tensor_tensor(out=out_b[:, q, :], in0=out_bank[:, 0:D],
                                             scalar=sum_b[:, q, 4:5], in1=x_big[:, u * 2 + q, :],
                                             op0=ALU.mult, op1=ALU.add).then_inc(b_out[q], 1)

                def off_small(u, q, i):
                    a = adj_small[q][:, i * H:(i + 1) * H]
                    dve.tensor_scalar(a, a, OFF_SCALE, None, ALU.mult, ALU.min,
                                      accum_out=off_min[:, q, i:i + 1]).then_inc(s_off[q], 1)

                def mask_small(u, q):
                    block_cols = adj_small[q][:, bass.ds((u * 2 + q) * P, P)]
                    dve.wait_ge(adj_s_in[q], u * 16 + 16)
                    dve.tensor_tensor(diag[:, q, :], block_cols, cap[:], ALU.min).then_inc(s_diag[q], 1)
                    dve.wait_ge(s_diag[q], u + 1)
                    dve.tensor_tensor(block_cols, block_cols, floor[:], ALU.max).then_inc(s_masked[q], 1)
                    dve.wait_ge(s_masked[q], u + 1)
                    off_small(u, q, 0)

                def out_small(u, q):
                    dve.wait_ge(adj_s_free[q], u + 2)
                    dve.tensor_reduce(sum_s[:, q, 3:4], sum_s[:, q, 0:3], AX.X, ALU.add
                                      ).then_inc(s_total[q], 1)
                    dve.wait_ge(s_total[q], u + 1)
                    dve.reciprocal(sum_s[:, q, 4:5], sum_s[:, q, 3:4]).then_inc(s_recip[q], 1)
                    dve.wait_ge(s_recip[q], u + 1)
                    dve.wait_ge(s_stored[q], u * 16 + 16)
                    dve.wait_ge(x_s_in[q], u * 16 + 16)
                    dve.wait_ge(s_opsum[q], u + 1)
                    dve.scalar_tensor_tensor(out=out_s[:, q, :], in0=m0[:, 0:D], scalar=sum_s[:, q, 4:5],
                                             in1=x_small[:, q, :], op0=ALU.mult, op1=ALU.add
                                             ).then_inc(s_out[q], 1)

                mask_small(0, 0)

                def body(u, q, up, un):
                    dve.wait_ge(s_qpsum[q], u + 1)
                    dve.tensor_tensor(Qs[:, q].rearrange("p c d -> p (c d)"), m1[:, 0:KD * P],
                                      c_wide[:].rearrange("p c d -> p (c d)"), ALU.add
                                      ).then_inc(s_q[q], 1)
                    dve.wait_ge(s_vpsum[q], u + 1)
                    dve.tensor_tensor(V32[:, q, :], m0[:, 0:DU], bias_row[:], ALU.add).then_inc(s_v[q], 1)
                    off_small(u, q, 1)
                    scores(u, q, 0)
                    scores(u, q, 1)
                    dve.wait_ge(s_off[q], u * 2 + 2)
                    dve.scalar_tensor_tensor(out=bound_s[:, q, 0:1], in0=off_min[:, q, 0:1],
                                             scalar=off_min[:, q, 1:2], in1=V32[:, q, D:DU],
                                             op0=ALU.min, op1=ALU.add).then_inc(s_offu[q], 1)
                    tiles = fixed(dve, u + 1)
                    dve.wait_ge(const_ready, 3)
                    dve.wait_ge(s_offu[q], tiles)
                    dve.wait_ge(s_spsum[q], tiles)
                    dve.tensor_tensor_reduce(diag[:, q, :], m0[:, 0:P], diag[:, q, :], -2.0,
                                             bound_s[:, q, 0:1], ALU.add, ALU.min, bound_s[:, q, 1:2]
                                             ).then_inc(s_bound[q], 1)
                    dve.wait_ge(s_bound[q], u + 1)
                    dve.tensor_tensor(bound_s[:, q, 2:3], bound_s[:, q, 1:2], V32[:, q, D:DU],
                                      ALU.subtract).then_inc(s_stat[q], 1)
                    if un is not None:
                        dve.wait_ge(x_s_in[1 - q], un * 16 + 16)
                        statistics(x_small[:, 1 - q, :], un + (1 - q), 1 - q)
                    scores(u, q, 2)
                    scores(u, q, 3)
                    dve.wait_ge(b_scores[q], u * NC + NC)
                    dve.tensor_tensor(bound_b[:, q, 6:7], bound_b[:, q, 5:6],
                                      u_big[:, bass.ds(u * 2 + q, 1)], ALU.subtract
                                      ).then_inc(b_stat[q], 1)
                    if un is not None:
                        normalize(x_small[:, 1 - q, :], un + (1 - q), 1 - q)
                        off_big(un, 1 - q)
                    out_small(u, q)
                    if un is not None:
                        mask_small(un, 1 - q)
                    if up is not None:
                        out_big(up, 1 - q)

                alternate(dve, NT, body)
                out_big(LAST, 1)
            with dve.Else():
                dve.wait_ge(g_ids, 2)
                dve.tensor_copy(g_ptr[:], ptr_row[:])
                dve.memset(g_graph[:], 0.0)
                dve.memset(g_rows[:], 0.0).then_inc(g_clear, 1)
                dve.wait_ge(g_clear, 1)
                with dve.Fori(0, NG) as i:
                    edge = g_ptr[:, bass.ds(i, 1)]
                    dve.scalar_tensor_tensor(out=g_graph[:], in0=g_key_id, scalar=edge, in1=g_graph[:],
                                             op0=ALU.is_ge, op1=ALU.add)
                    dve.scalar_tensor_tensor(out=g_rows[:], in0=g_row_id[:], scalar=edge,
                                             in1=g_rows[:], op0=ALU.is_ge, op1=ALU.add
                                             ).then_inc(g_clear, 1)
                    dve.wait_ge(g_clear, i + 2)

                with dve.Fori(0, GT) as t:
                    dve.wait_ge(x_s_in[0], t * 16 + 16)
                    statistics(x_small[:, 0, :], t + 1, 0)
                    normalize(x_small[:, 0, :], t + 1, 0)
                    dve.wait_ge(s_vpsum[0], t + 1)
                    dve.tensor_tensor(g_V[:, t, :], m1[:, 0:DU], bias_row[:], ALU.add
                                      ).then_inc(s_v[0], 1)
                dve.wait_ge(s_v[0], GT)
                dve.sem_inc(g_graphs, 1)

                with dve.Fori(0, GT) as t:
                    steps = [0]

                    def step(ins):
                        ins.then_inc(g_step, 1)
                        steps[0] += 1
                        dve.wait_ge(g_step, t * G_STEPS + steps[0])

                    dve.wait_ge(s_qpsum[0], t + 1)
                    dve.tensor_tensor(Qs[:, 0].rearrange("p c d -> p (c d)"), m1[:, 0:KD * P],
                                      c_wide[:].rearrange("p c d -> p (c d)"), ALU.add
                                      ).then_inc(s_q[0], 1)
                    step(dve.tensor_copy(g_row[:, 0:1], g_rows[:, bass.ds(t, 1)]))
                    step(dve.tensor_copy(g_row[:, 1:2], g_V[:, t, D:DU]))
                    step(dve.tensor_scalar(g_in[:], g_graph[:], g_row[:, 0:1], 2 * FARTHEST,
                                           ALU.is_equal, ALU.mult))
                    step(dve.tensor_scalar(g_in[:], g_in[:], -FARTHEST, None, ALU.add))
                    dve.wait_ge(g_adj_in, t * 16 + 16)
                    step(dve.tensor_scalar(g_z[:], g_adj[:], OFF_SCALE, g_row[:, 1:2], ALU.mult,
                                           ALU.add))
                    step(dve.scalar_tensor_tensor(out=g_z[:], in0=g_in[:], scalar=-1.0, in1=g_z[:],
                                                  op0=ALU.mult, op1=ALU.min))
                    for c in range(GC):
                        dve.wait_ge(g_spsum, t * GC + (c + 1))
                        a = g_adj[:, c * CH:(c + 1) * CH]
                        step(dve.tensor_tensor(a, score_bank[c % 2][:], a, ALU.add))
                    step(dve.scalar_tensor_tensor(out=g_adj[:], in0=g_adj[:], scalar=-2.0,
                                                  in1=g_in[:], op0=ALU.mult, op1=ALU.min))
                    step(dve.tensor_tensor(g_z[:], g_z[:], g_adj[:], ALU.max))
                    step(dve.tensor_reduce(g_row[:, 2:3], g_z[:], AX.X, ALU.min))
                    assert steps[0] == G_BOUND
                    dve.wait_ge(g_exp, t + 1)
                    step(dve.scalar_tensor_tensor(out=g_z[:], in0=g_in[:], scalar=0.0, in1=g_z[:],
                                                  op0=ALU.is_gt, op1=ALU.mult))
                    step(dve.tensor_reduce(g_sum[:, GC:GC + 1], g_sum[:, 0:GC], AX.X, ALU.add))
                    step(dve.reciprocal(g_sum[:, GC + 1:GC + 2], g_sum[:, GC:GC + 1]))
                    dve.wait_ge(g_opsum, t + 1)
                    dve.wait_ge(g_x_in, t * 16 + 16)
                    step(dve.tensor_scalar(out_s[:, 0, :], out_bank[:, 0:D],
                                           g_sum[:, GC + 1:GC + 2], None, ALU.mult))
                    step(dve.tensor_tensor(out_s[:, 0, :], out_s[:, 0, :], x_small[:, 1, :], ALU.add))
                    assert steps[0] == G_STEPS
                    dve.sem_inc(g_out, 1)

        @block.tensor
        def _(pe):
            pe.wait_ge(w_in, 6 * 16)
            pe.wait_ge(ident_ready, 2)
            for i in range(KD):
                for o in range(KD):
                    last = pe.transpose(m1[:, i * D + o * P:i * D + (o + 1) * P],
                                        Wv_sb[:, o, i * P:(i + 1) * P], ident[:])
            last.then_inc(prep_psum, 1)
            pe.wait_ge(w_wide, 1)
            for k, (w, b) in enumerate(((Wk_sb, bq_col), (Wq_sb, bk_col))):
                for i in range(KD):
                    for o in range(KD):
                        pe.matmul(out_bank[:, k * KD + i:k * KD + i + 1], w[:, o, i * P:(i + 1) * P],
                                  b[:, o:o + 1], start=(o == 0), stop=(o == KD - 1))
            for o in range(KD):
                last = pe.matmul(out_bank[:, 2 * KD:2 * KD + 1], bq_wide[:, o, :], bk_col[:, o:o + 1],
                                 start=(o == 0), stop=(o == KD - 1))
            last.then_inc(prep_psum, 1)
            for i in range(KD):
                for o in range(KD):
                    last = pe.matmul(m0[:, i * D:(i + 1) * D], Wq_sb[:, o, i * P:(i + 1) * P],
                                     Wk_sb[:, o, :], start=(o == 0), stop=(o == KD - 1))
            last.then_inc(G_psum, 1)
            pe.wait_ge(prep_done, 2)

            def turn(bank, q, done):
                for c in range(KD):
                    last = pe.transpose(bank[:, c * P:(c + 1) * P], xn[:, q, c * P:(c + 1) * P],
                                        ident[:])
                last.then_inc(done[q], 1)

            def project_v(bank, q, done):
                for c in range(KD):
                    last = pe.matmul(bank[:, 0:DU], hT[:, q, c, :], WvT[:, c, :], start=(c == 0),
                                     stop=(c == KD - 1))
                last.then_inc(done[q], 1)

            with pe.If(regular_ptr(pe)):
                def turn_big(u, q):
                    pe.wait_ge(p_lo[q], u + 1)
                    pe.wait_ge(p_xn[q], u + 1)
                    for c in range(KD):
                        for i in range(2):
                            last = pe.transpose(score_bank[q][:, (c * 2 + i) * P:(c * 2 + i + 1) * P],
                                                xn_two[q][:, i, c * P:(c + 1) * P], ident[:])
                    last.then_inc(p_turned[q], 1)

                def before(u, q, up, un):
                    if un is not None:
                        turn_big(un, 1 - q)
                    pe.wait_ge(p_v32[q], u + 1)
                    pe.wait_ge(p_h32[q], u + 1)
                    for i in range(2):
                        for c in range(KD):
                            last = pe.matmul(V_two_bank[q][i][:, 0:DU],
                                             hT_two[q][:, (c * 2 + i) * P:(c * 2 + i + 1) * P],
                                             WvT[:, c, :], start=(c == 0), stop=(c == KD - 1))
                    last.then_inc(p_vpsum[q], 1)

                turn_big(0, 0)
                alternate(pe, NT // 2, before)

                def q_big(u, q):
                    for j in range(KD):
                        k = 0
                        for c in range(KD):
                            for g, h in ((G_hi, hT_hi), (G_hi, hT_lo), (G_lo, hT_hi)):
                                last = pe.matmul(m1[:, j * P:(j + 1) * P], g[:, c, j * P:(j + 1) * P],
                                                 h[:, c, bass.ds((u * 2 + q) * P, P)], start=(k == 0),
                                                 stop=(k == 3 * KD - 1))
                                k += 1
                    last.then_inc(b_qpsum[q], 1)

                pe.wait_ge(G_step, 3)
                pe.wait_ge(p_lo[0], NT // 4 + 1)
                pe.wait_ge(p_lo[1], NT // 4 + 1)
                q_big(0, 0)
                pe.wait_ge(b_q32[0], 1)
                pe.wait_ge(p_vlo[0], NT // 4 + 1)
                pe.wait_ge(p_vlo[1], NT // 4 + 1)

                def score_chunk(u, q, c):
                    if c == 3:
                        pe.wait_ge(b_scores[q], u * NC + 1)
                    k = 0
                    for j in range(KD):
                        for a, h in ((Qb_hi, hT_hi), (Qb_hi, hT_lo), (Qb_lo, hT_hi)):
                            last = pe.matmul(score_bank[c % 3][:], a[:, q, j, :],
                                             h[:, j, c * CH:(c + 1) * CH], start=(k == 0),
                                             stop=(k == 3 * KD - 1))
                            k += 1
                    last.then_inc(b_spsum[q], 1)

                def turn_probs(u, q, c):
                    pe.wait_ge(b_probs[q], u * 2 + (1 + c // 2))
                    if c >= 2:
                        pe.wait_ge(b_pT32[q], u * NC + (c - 1))
                    for k in range(KB):
                        last = pe.transpose(turn_bank[c % 2][:, k * P:(k + 1) * P],
                                            probs[:, (c * KB + k) * P:(c * KB + k + 1) * P], ident[:])
                    last.then_inc(b_tpsum[q], 1)

                def attend(u, q, c):
                    pe.wait_ge(b_pT[q], u * NC + (c + 1))
                    for k in range(KB):
                        b = c * KB + k
                        s = slice(k * P, (k + 1) * P)
                        for i, (a, v) in enumerate(((PT_hi, V_hi), (PT_hi, V_lo), (PT_lo, V_hi))):
                            last = pe.matmul(out_bank[:, 0:D], a[:, c, s], v[:, b, :],
                                             start=(b == 0 and i == 0), stop=(b == NT - 1 and i == 2))
                    last.then_inc(b_pv[q], 1)

                pe.wait_ge(xn_ready[0], 1)
                turn(m1, 0, s_turned)

                def body(u, q, up, un):
                    pe.wait_ge(s_hT[q], u + 1)
                    for j in range(KD):
                        for c in range(KD):
                            last = pe.matmul(m1[:, j * P:(j + 1) * P], G32[:, c, j * P:(j + 1) * P],
                                             hT[:, q, c, :], start=(c == 0), stop=(c == KD - 1))
                    last.then_inc(s_qpsum[q], 1)
                    if up is not None:
                        pe.wait_ge(s_out[1 - q], up + 2)
                    project_v(m0, q, s_vpsum)
                    pe.wait_ge(b_q[q], u + 1)
                    if up is not None:
                        pe.wait_ge(b_scores[1 - q], up * NC + NC)
                    score_chunk(u, q, 0)
                    score_chunk(u, q, 1)
                    pe.wait_ge(s_q[q], u + 1)
                    pe.wait_ge(s_v[q], u + 1)
                    for c in range(KD):
                        last = pe.matmul(m0[:, 0:P], Qs[:, q, c, :], hT[:, q, c, :], start=(c == 0),
                                         stop=(c == KD - 1))
                    last.then_inc(s_spsum[q], 1)
                    if un is not None:
                        q_big(un, 1 - q)
                    score_chunk(u, q, 2)
                    score_chunk(u, q, 3)
                    pe.wait_ge(s_probs[q], u + 1)
                    if un is not None:
                        pe.wait_ge(b_q32[1 - q], un + 1)
                    pe.transpose(m1[:, 0:P], diag[:, q, :], ident[:]).then_inc(s_tpsum[q], 1)
                    if up is not None:
                        pe.wait_ge(b_out[q], u + 1)
                        attend(up, 1 - q, 0)
                        attend(up, 1 - q, 1)
                    pe.wait_ge(s_pT[q], u + 1)
                    pe.wait_ge(s_stat[q], u + 1)
                    pe.matmul(m0[:, 0:D], PsT[:, q, :], V32[:, q, 0:D], start=True, stop=True
                              ).then_inc(s_opsum[q], 1)
                    if un is not None:
                        pe.wait_ge(xn_ready[1 - q], un + 1)
                        turn(m1, 1 - q, s_turned)
                    for c in range(NC):
                        turn_probs(u, q, c)
                        if c == 1 and up is not None:
                            attend(up, 1 - q, 2)
                            attend(up, 1 - q, 3)

                alternate(pe, NT, body)
                pe.wait_ge(b_out[0], LAST + 2)
                for c in range(NC):
                    attend(LAST, 1, c)
            with pe.Else():
                pe.wait_ge(G_step, 1)
                with pe.Fori(0, GT) as t:
                    pe.wait_ge(xn_ready[0], t + 1)
                    turn(m0, 0, s_turned)
                    pe.wait_ge(s_hT[0], t + 1)
                    project_v(m1, 0, s_vpsum)
                    pe.wait_ge(s_v[0], t + 1)
                with pe.Fori(0, GT) as t:
                    for j in range(KD):
                        for c in range(KD):
                            last = pe.matmul(m1[:, j * P:(j + 1) * P], G32[:, c, j * P:(j + 1) * P],
                                             g_hT[:, c, bass.ds(t * P, P)], start=(c == 0),
                                             stop=(c == KD - 1))
                    last.then_inc(s_qpsum[0], 1)
                    pe.wait_ge(s_q[0], t + 1)
                    for c in range(GC):
                        if c >= 2:
                            pe.wait_ge(g_step, t * G_STEPS + (5 + c))
                        for j in range(KD):
                            last = pe.matmul(score_bank[c % 2][:], Qs[:, 0, j, :],
                                             g_hT[:, j, c * CH:(c + 1) * CH], start=(j == 0),
                                             stop=(j == KD - 1))
                        last.then_inc(g_spsum, 1)
                    pe.wait_ge(g_step, t * G_STEPS + (G_BOUND + 1))
                    for c in range(GC):
                        if c >= 2:
                            pe.wait_ge(g_turned, t * GC + (c - 1))
                        for k in range(KB):
                            b = c * KB + k
                            last = pe.transpose(turn_bank[c % 2][:, k * P:(k + 1) * P],
                                                g_z[:, b * P:(b + 1) * P], ident[:])
                        last.then_inc(g_tpsum, 1)
                    pe.wait_ge(g_turned, t * GC + GC)
                    for b in range(GT):
                        last = pe.matmul(out_bank[:, 0:D], g_adj[:, b * P:(b + 1) * P],
                                         g_V[:, b, 0:D], start=(b == 0), stop=(b == GT - 1))
                    last.then_inc(g_opsum, 1)
                    pe.wait_ge(g_out, t + 1)


_INS = ['x', 'adj', 'L0_gnn_ptr', 'L0_gnn_Wq', 'L0_gnn_bq', 'L0_gnn_Wk', 'L0_gnn_bk', 'L0_gnn_Wv', 'L0_gnn_bv']


def kernel(**inputs):
    import numpy as _np
    import concourse.bacc as _bacc
    from concourse import mybir as _mybir
    from concourse.bass_utils import run_bass_kernel_spmd as _run

    nc = _bacc.Bacc("TRN2", target_bir_lowering=False, num_devices=1)
    arrays, args = {}, []
    for name in _INS:
        a = _np.ascontiguousarray(inputs[name])
        arrays[f"in_{name}"] = a
        args.append(nc.dram_tensor(f"in_{name}", a.shape, _mybir.dt.from_np(a.dtype), kind="ExternalInput").ap())
    shape = inputs['x'].shape
    args.append(nc.dram_tensor("out_0", shape, _mybir.dt.float32, kind="ExternalOutput").ap())
    build_program(nc, *args)
    r = _run(nc, [arrays], core_ids=[0])
    return r.results[0]["out_0"]
```

```python
from contextlib import ExitStack

import concourse.bass as bass
from concourse import mybir

P = 128
BIG = 3.0e38
FAR = 1.0e30
FARTHEST = 1.5e38
OFF_SCALE = 2.0e6
EPS = 1e-5

ALU = mybir.AluOpType
ACT = mybir.ActivationFunctionType
AX = mybir.AxisListType
F32 = mybir.dt.float32
F32R = mybir.dt.float32r
I32 = mybir.dt.int32


def build_program(nc, x, adj, ptr, Wq, bq, Wk, bk, Wv, bv, out):
    N, D = x.shape
    H = N // 2
    NT = H // P
    NG = ptr.shape[0]
    GS = H // (ptr.shape[0] - 1)
    KD = D // P
    CH = 512
    NC = H // CH
    KB = CH // P
    GT = N // P
    GC = N // CH
    DU = D + 1
    SC = 1.0 / float(D) ** 0.5

    with ExitStack() as ctx:
        def sb(name, shape, dt=F32, to=ctx):
            return to.enter_context(nc.sbuf_tensor(name, shape, dt))

        def ps(name):
            return ctx.enter_context(nc.psum_tensor(name, [P, 512], F32))

        def sem(name):
            return ctx.enter_context(nc.semaphore(name))

        def sem2(name):
            return [sem(name + "0"), sem(name + "1")]

        score_bank = [ps(f"score_bank{i}") for i in range(3)]
        turn_bank = [ps(f"turn_bank{i}") for i in range(2)]
        out_bank = ps("out_bank")
        small_bank = ps("small_bank")
        query_bank = ps("query_bank")
        G_bank = [small_bank, score_bank[2]]

        x_big = sb("x_big", [P, NT, D])
        x_small = sb("x_small", [P, 2, D])
        probs = sb("probs", [P, H])
        G32 = sb("G32", [P, KD, D])
        WvT = sb("WvT", [P, KD, DU])
        bias_row = sb("bias_row", [P, DU])
        c_col = sb("c_col", [P, KD])
        c_wide = sb("c_wide", [P, KD, P])
        ident = sb("ident", [P, P])
        cap = sb("cap", [P, P])
        floor = sb("floor", [P, P])
        bq_col = sb("bq_col", [P, KD])
        half = sb("half", [P, 1])

        def in_probs(at, width):
            return probs[:, at:at + KD * width].rearrange("p (c d) -> p c d", c=KD)

        Wq_sb, Wv_sb = in_probs(0, D), in_probs(KD * D, D)
        Wk_bk = in_probs(2 * KD * D, DU)
        bq_wide = in_probs(2 * KD * D + KD * DU, P)
        moments_two = sb("moments_two", [P, 2, 2, 6])
        mean_var_two = sb("mean_var_two", [P, 2, 2, 2])
        var_eps_two = sb("var_eps_two", [P, 2, 2])
        rstd_two = sb("rstd_two", [P, 2, 2])
        ptr_row = sb("ptr_row", [P, NG], I32)
        ptr_drawn = sb("ptr_drawn", [P, NG], I32)
        ptr_same = sb("ptr_same", [P, NG])
        path = sb("path", [P, 1], I32)
        moments = sb("moments", [P, 2, 6])
        mean_var = sb("mean_var", [P, 2, 2])
        var_eps = sb("var_eps", [P, 2])
        rstd = sb("rstd", [P, 2])
        xn = sb("xn", [P, 2, D])
        hT = sb("hT", [P, 2, KD, P])
        V32 = sb("V32", [P, 2, DU])
        Qs = sb("Qs", [P, 2, KD, P])
        out_s = sb("out_s", [P, 2, D])

        with ExitStack() as regular:
            adj_big = [sb(f"adj_big{i}", [P, N], to=regular) for i in range(2)]
            adj_small = [sb(f"adj_small{i}", [P, N], to=regular) for i in range(2)]
            hT_hi = sb("hT_hi", [P, KD, H], F32R, to=regular)
            hT_lo = sb("hT_lo", [P, KD, H], F32R, to=regular)
            V_hi = sb("V_hi", [P, NT, D], F32R, to=regular)
            V_lo = sb("V_lo", [P, NT, D], F32R, to=regular)
            u_big = sb("u_big", [P, NT], to=regular)
            PT32 = sb("PT32", [P, 2, CH], to=regular)
            PT_hi = sb("PT_hi", [P, NC, CH], F32R, to=regular)
            PT_lo = sb("PT_lo", [P, NC, CH], F32R, to=regular)
            G_hi = sb("G_hi", [P, KD, D], F32R, to=regular)
            G_lo = sb("G_lo", [P, KD, D], F32R, to=regular)
            Qb32 = sb("Qb32", [P, 2, KD, P], to=regular)
            Qb_hi = sb("Qb_hi", [P, 2, KD, P], F32R, to=regular)
            Qb_lo = sb("Qb_lo", [P, 2, KD, P], F32R, to=regular)
            diag = sb("diag", [P, 2, P], to=regular)
            PsT = sb("PsT", [P, 2, P], to=regular)
            off_min = sb("off_min", [P, 2, 2], to=regular)
            bound_s = sb("bound_s", [P, 2, 3], to=regular)
            bound_b = sb("bound_b", [P, 2, 7], to=regular)
            sum_s = sb("sum_s", [P, 2, 5], to=regular)
            sum_b = sb("sum_b", [P, 2, 5], to=regular)
            out_b = sb("out_b", [P, 2, D], to=regular)
            xn_two = [xn[:], PT32[:, 0, :].rearrange("p (i d) -> p i d", i=2)]
            hT_two = [hT[:].rearrange("p a b q -> p (a b q)"), out_b[:].rearrange("p i d -> p (i d)")]
            bias_hi, ones = PT_hi[:, 0, 0:D], PT_hi[:, 1, 0:P]
            bias_lo = PT_lo[:, 0, 0:D]
            V_two_bank = [turn_bank, [out_bank, small_bank]]

        with ExitStack() as general:
            g_hT = sb("g_hT", [P, KD, N], to=general)
            g_V = sb("g_V", [P, N // P, DU], to=general)
            g_graph = sb("g_graph", [P, N], to=general)
            g_adj = sb("g_adj", [P, N], to=general)
            g_in = sb("g_in", [P, N], to=general)
            g_z = sb("g_z", [P, N], to=general)
            g_rows = sb("g_rows", [P, N // P], to=general)
            g_row_id = sb("g_row_id", [P, N // P], I32, to=general)
            g_ptr = sb("g_ptr", [P, NG], to=general)
            g_row = sb("g_row", [P, 3], to=general)
            g_sum = sb("g_sum", [P, GC + 2], to=general)
            g_key_id = g_z[:].bitcast(I32)

        w_in = sem("w_in")
        x_in = [sem("x_in_first"), sem("x_in_rest")]
        ptr_in = sem("ptr_in")
        ptr_id = sem("ptr_id")
        ptr_step = sem("ptr_step")
        path_known = sem("path_known")
        w_wide = sem("w_wide")
        const_ready = sem("const_ready")
        ident_ready = sem("ident_ready")
        prep_psum = sem("prep_psum")
        wvt_done = sem("wvt_done")
        u_done = sem("u_done")
        c_done = sem("c_done")
        c_spread = sem("c_spread")
        G_psum = sem("G_psum")
        G_step = sem("G_step")
        g_clear = sem("g_clear")
        moments_done = sem2("moments_done")
        mean_done = sem2("mean_done")
        var_ready = sem2("var_ready")
        rstd_ready = sem2("rstd_ready")
        xn_ready = sem2("xn_ready")
        bias_step = sem("bias_step")
        p_moments = sem2("p_moments")
        p_mean = sem2("p_mean")
        p_var = sem2("p_var")
        p_rstd = sem2("p_rstd")
        p_xn = sem2("p_xn")
        p_turned = sem2("p_turned")
        p_h32 = sem2("p_h32")
        p_hi = sem2("p_hi")
        p_lo = sem2("p_lo")
        p_vpsum = sem2("p_vpsum")
        p_vhi = sem2("p_vhi")
        p_vlo = sem2("p_vlo")
        adj_b_in = sem2("adj_b_in")
        adj_o_in = sem2("adj_o_in")
        adj_s_in = sem2("adj_s_in")
        x_s_in = sem2("x_s_in")
        adj_b_free = sem2("adj_b_free")
        adj_s_free = [sem2("adj_s_lower_free"), sem2("adj_s_upper_free")]
        s_turned = sem2("s_turned")
        s_hT = sem2("s_hT")
        s_qpsum = sem2("s_qpsum")
        s_vpsum = sem2("s_vpsum")
        s_q = sem2("s_q")
        s_v = sem2("s_v")
        s_spsum = sem2("s_spsum")
        s_diag = sem2("s_diag")
        s_masked = sem2("s_masked")
        s_off = sem2("s_off")
        s_offu = sem2("s_offu")
        s_bound = sem2("s_bound")
        s_stat = sem2("s_stat")
        s_probs = sem2("s_probs")
        s_tpsum = sem2("s_tpsum")
        s_pT = sem2("s_pT")
        s_opsum = sem2("s_opsum")
        s_total = sem2("s_total")
        s_recip = sem2("s_recip")
        s_out = sem2("s_out")
        s_stored = sem2("s_stored")
        b_qpsum = sem("b_qpsum")
        b_q32 = sem("b_q32")
        b_qhi = sem2("b_qhi")
        b_q = sem2("b_q")
        b_off = sem2("b_off")
        b_offu = sem2("b_offu")
        b_spsum = sem2("b_spsum")
        b_scores = sem2("b_scores")
        b_stat = sem2("b_stat")
        b_probs = sem2("b_probs")
        b_tpsum = sem2("b_tpsum")
        b_pT32 = sem2("b_pT32")
        b_pT = sem2("b_pT")
        b_pv = sem2("b_pv")
        b_total = sem2("b_total")
        b_recip = sem2("b_recip")
        b_out = sem2("b_out")
        b_stored = sem2("b_stored")

        g_ids = sem("g_ids")
        g_graphs = sem("g_graphs")
        g_adj_in = sem("g_adj_in")
        g_step = sem("g_step")
        g_exp = sem("g_exp")
        g_spsum = sem("g_spsum")
        g_tpsum = sem("g_tpsum")
        g_turned = sem("g_turned")
        g_opsum = sem("g_opsum")
        g_out = sem("g_out")
        g_stored = sem("g_stored")
        g_x_in = sem("g_x_in")

        LAST = NT // 2 - 1
        TWO = NT // 4
        FIRST = 4
        G_BOUND = GC + 9
        G_STEPS = G_BOUND + 5

        def regular_ptr(eng):
            eng.wait_ge(path_known, 1)
            return eng.value_load(path[0:1, 0:1], min_val=0, max_val=1) == 1

        def fixed(eng, value):
            return value if isinstance(value, int) else eng.to_reg(value)

        def alternate(eng, count, body):
            last = count // 2 - 1
            body(0, 0, None, 0)
            with eng.Fori(0, last) as it:
                body(it, 1, it, it + 1)
                body(it + 1, 0, it, it + 1)
            body(last, 1, last, None)

        block = ctx.enter_context(nc.Block())

        @block.sync
        def _(sp):
            sp.dma_start(ptr_row[:], ptr.rearrange("(a d) -> a d", a=1).broadcast_to([P, NG])
                         ).then_inc(ptr_in, 16)
            for w, dst in ((Wq, Wq_sb), (Wk, Wk_bk[:, :, 0:D]), (Wv, Wv_sb)):
                sp.dma_start(dst, w.rearrange("(c p) d -> p c d", p=P)).then_inc(w_in, 16)
            sp.dma_start(bq_col[:], bq.rearrange("(c p) -> p c", p=P),
                         allow_slow_non_contiguous=True).then_inc(w_in, 16)
            sp.dma_start(Wk_bk[:, :, D], bk.rearrange("(c p) -> p c", p=P),
                         allow_slow_non_contiguous=True).then_inc(w_in, 16)
            sp.dma_start(bias_row[:, 0:D], bv.rearrange("(a d) -> a d", a=1).broadcast_to([P, D])
                         ).then_inc(w_in, 16)
            for i, (a, b) in enumerate(((0, FIRST), (FIRST, NT))):
                rows = x[H + a * P:H + b * P, :]
                sp.dma_start(x_big[:, a:b, :], rows.rearrange("(t p) d -> p t d", p=P)
                             ).then_inc(x_in[i], 16)

            with sp.If(regular_ptr(sp)):
                def load(u, q):
                    n = u * 2 + q
                    inside, outside = slice(H, N), slice(0, H)
                    small, big = adj[bass.ds(n * P, P), :], adj[bass.ds(n * P + H, P), :]
                    sp.wait_ge(path_known, 1)
                    sp.wait_ge(adj_s_free[0][q], u + 1)
                    sp.dma_start(adj_small[q][:, 0:H], small[:, 0:H]).then_inc(adj_s_in[q], 16)
                    sp.wait_ge(path_known, 1)
                    sp.wait_ge(b_probs[q], u * 2 + 1)
                    sp.dma_start(adj_big[q][:, inside], big[:, inside]).then_inc(adj_b_in[q], 16)
                    sp.wait_ge(path_known, 1)
                    sp.wait_ge(adj_s_free[1][q], u + 1)
                    sp.dma_start(adj_small[q][:, H:N], small[:, H:N]).then_inc(adj_s_in[q], 16)
                    sp.wait_ge(path_known, 1)
                    sp.wait_ge(s_out[q], u + 1)
                    sp.dma_start(x_small[:, q, :], x[bass.ds(n * P, P), :]).then_inc(x_s_in[q], 16)
                    sp.wait_ge(path_known, 1)
                    sp.wait_ge(adj_b_free[q], u + 1)
                    sp.dma_start(adj_big[q][:, outside], big[:, outside]).then_inc(adj_o_in[q], 16)

                def store_small(u, q):
                    sp.wait_ge(path_known, 1)
                    sp.wait_ge(s_out[q], u + 2)
                    sp.dma_start(out[bass.ds((u * 2 + q) * P, P), :], out_s[:, q, :]
                                 ).then_inc(s_stored[q], 16)

                def store_big(u, q):
                    sp.wait_ge(path_known, 1)
                    sp.wait_ge(b_out[q], u + 2)
                    sp.dma_start(out[bass.ds((u * 2 + q) * P + H, P), :], out_b[:, q, :]
                                 ).then_inc(b_stored[q], 16)

                load(0, 0)
                load(0, 1)
                load(1, 0)
                store_small(0, 0)
                load(1, 1)
                store_small(0, 1)
                store_big(0, 0)
                with sp.Fori(2, NT // 2) as u:
                    load(u, 0)
                    store_small(u - 1, 0)
                    store_big(u - 2, 1)
                    load(u, 1)
                    store_small(u - 1, 1)
                    store_big(u - 1, 0)
                store_big(LAST - 1, 1)
                store_small(LAST, 0)
                store_big(LAST, 0)
                store_small(LAST, 1)
                store_big(LAST, 1)
                for q in range(2):
                    sp.wait_ge(s_stored[q], 16 * (NT // 2 + 1))
                    sp.wait_ge(b_stored[q], 16 * (NT // 2 + 1))
            with sp.Else():
                def g_rows_of(a, t):
                    return a[bass.ds(t * P, P), :]

                sp.dma_start(x_small[:, 0, :], g_rows_of(x, 0)).then_inc(x_s_in[0], 16)
                with sp.Fori(1, GT) as t:
                    sp.wait_ge(xn_ready[0], t)
                    sp.dma_start(x_small[:, 0, :], g_rows_of(x, t)).then_inc(x_s_in[0], 16)
                sp.wait_ge(g_graphs, 1)
                sp.dma_start(g_adj[:], g_rows_of(adj, 0)).then_inc(g_adj_in, 16)
                sp.dma_start(x_small[:, 1, :], g_rows_of(x, 0)).then_inc(g_x_in, 16)
                with sp.Fori(1, GT) as t:
                    sp.wait_ge(g_out, t)
                    sp.dma_start(g_rows_of(out, t - 1), out_s[:, 0, :]).then_inc(g_stored, 16)
                    sp.wait_ge(g_stored, t * 16)
                    sp.dma_start(g_adj[:], g_rows_of(adj, t)).then_inc(g_adj_in, 16)
                    sp.dma_start(x_small[:, 1, :], g_rows_of(x, t)).then_inc(g_x_in, 16)
                sp.wait_ge(g_out, GT)
                sp.dma_start(g_rows_of(out, GT - 1), out_s[:, 0, :]).then_inc(g_stored, 16)
                sp.wait_ge(g_stored, GT * 16)

        @block.scalar
        def _(act):
            for q in range(2):
                act.sem_inc(adj_s_free[0][q], 1)
                act.sem_inc(adj_s_free[1][q], 1)
                act.sem_inc(b_probs[q], 1)
                act.sem_inc(adj_b_free[q], 1)
                act.sem_inc(p_hi[q], 1)
            act.wait_ge(prep_psum, 1)
            act.activation(WvT[:, :, 0:D], query_bank[:, 0:KD * D].rearrange("p (c d) -> p c d", c=KD),
                           ACT.Copy).then_inc(wvt_done, 1)
            act.wait_ge(G_psum, 1)
            act.activation(c_col[:], query_bank[:, 0:KD], ACT.Copy, scale=SC / 2).then_inc(c_done, 1)
            act.wait_ge(c_done, 1)
            for c in range(KD):
                last = act.activation(c_wide[:, c, :], ident[:], ACT.Identity,
                                      bias=c_col[:, c:c + 1], scale=0.0)
            last.then_inc(c_spread, 1)
            act.wait_ge(G_psum, 2)
            for i in range(KD):
                last = act.activation(G32[:, i, :], G_bank[i][:, 0:D], ACT.Copy, scale=SC / 2)
            last.then_inc(G_step, 1)

            with act.If(regular_ptr(act)):
                def turn_in(u, q):
                    act.wait_ge(p_lo[q], u + 1)
                    act.wait_ge(p_turned[q], u + 1)
                    src = score_bank[q][:]
                    act.activation(hT_two[q], src, ACT.Relu).then_inc(p_h32[q], 1)
                    act.activation(hT_hi[:, :, bass.ds((u * 2 + q) * 2 * P, 2 * P)],
                                   src.rearrange("p (c d) -> p c d", c=KD), ACT.Relu
                                   ).then_inc(p_hi[q], 1)

                def q_big(u):
                    act.wait_ge(b_qpsum, u + 1)
                    for j in range(KD):
                        last = act.activation(Qb32[:, :, j, :],
                                              query_bank[:, j * 2 * P:(j + 1) * 2 * P].rearrange(
                                                  "p (q d) -> p q d", q=2),
                                              ACT.Identity, bias=c_col[:, j:j + 1])
                    last.then_inc(b_q32, 1)

                def before(u, q, up, un):
                    if un is not None:
                        turn_in(un, 1 - q)
                    else:
                        q_big(0)
                    twos = fixed(act, u + 1)
                    act.wait_ge(wvt_done, 1)
                    act.wait_ge(p_vpsum[q], twos)
                    for i in range(2):
                        last = act.activation(V_hi[:, bass.ds((u * 2 + q) * 2 + i, 1), :],
                                              V_two_bank[q][i][:, 0:D].rearrange("p (i d) -> p i d", i=1),
                                              ACT.Copy)
                    last.then_inc(p_vhi[q], 1)

                for i in range(KD):
                    last = act.activation(G_hi[:, i, :], G_bank[i][:, 0:D], ACT.Copy, scale=SC / 2)
                last.then_inc(G_step, 1)
                turn_in(0, 0)
                alternate(act, NT // 2, before)

                def turn_in_small(u, q):
                    act.wait_ge(s_turned[q], u + 1)
                    act.activation(hT[:, q].rearrange("p c d -> p (c d)"), query_bank[:, 0:D], ACT.Relu
                                   ).then_inc(s_hT[q], 1)

                act.wait_ge(p_lo[0], TWO + 1)
                turn_in_small(0, 0)

                def off_small(q, i):
                    a = adj_small[q][:, i * H:(i + 1) * H]
                    act.activation(a, a, ACT.Exp, bias=bound_s[:, q, 2:3], scale=-1.0,
                                   accum_out=sum_s[:, q, 1 + i:2 + i]
                                   ).then_inc(adj_s_free[i][q], 1)

                def exp_big(q, i):
                    act.activation(probs[:, i * H // 2:(i + 1) * H // 2],
                                   adj_big[q][:, H + i * H // 2:H + (i + 1) * H // 2], ACT.Exp,
                                   bias=bound_b[:, q, 5:6], scale=-1.0,
                                   accum_out=sum_b[:, q, i:i + 1]).then_inc(b_probs[q], 1)

                def exp_small(u, q):
                    act.wait_ge(s_stat[q], u + 1)
                    act.activation(diag[:, q, :], diag[:, q, :], ACT.Exp, bias=bound_s[:, q, 1:2],
                                   scale=-1.0, accum_out=sum_s[:, q, 0:1]).then_inc(s_probs[q], 1)

                def body(u, q, up, un):
                    exp_small(u, q)
                    if q == 1 and un is not None:
                        q_big(un)
                    off_small(q, 0)
                    act.wait_ge(s_tpsum[q], u + 1)
                    act.copy(PsT[:, q, :], query_bank[:, 0:P]).then_inc(s_pT[q], 1)
                    act.wait_ge(b_stat[q], u + 1)
                    exp_big(q, 0)
                    exp_big(q, 1)
                    if un is not None:
                        turn_in_small(un, 1 - q)
                    for c in range(NC):
                        act.wait_ge(b_tpsum[q], u * NC + (c + 1))
                        if up is not None:
                            act.wait_ge(b_pv[1 - q], up * NC + (c + 1))
                        act.copy(PT_hi[:, c, :], turn_bank[c % 2][:])
                        if c >= 2:
                            act.wait_ge(b_pT[q], u * NC + (c - 1))
                        elif up is not None:
                            act.wait_ge(b_pT[1 - q], up * NC + (c + 3))
                        act.copy(PT32[:, c % 2, :], turn_bank[c % 2][:]).then_inc(b_pT32[q], 1)
                        if c == (1 if un is not None else NC - 1):
                            off_small(q, 1)
                    act.activation(adj_big[q][:, 0:H], adj_big[q][:, 0:H], ACT.Exp,
                                   bias=bound_b[:, q, 6:7], scale=-1.0,
                                   accum_out=sum_b[:, q, 2:3]).then_inc(adj_b_free[q], 1)

                alternate(act, NT, body)
            with act.Else():
                with act.Fori(0, GT) as t:
                    act.wait_ge(s_turned[0], t + 1)
                    act.activation(hT[:, 0].rearrange("p c d -> p (c d)"), small_bank[:, 0:D], ACT.Relu)
                    act.activation(g_hT[:, :, bass.ds(t * P, P)],
                                   small_bank[:, 0:D].rearrange("p (c d) -> p c d", c=KD), ACT.Relu
                                   ).then_inc(s_hT[0], 1)
                with act.Fori(0, GT) as t:
                    act.wait_ge(g_step, t * G_STEPS + G_BOUND)
                    for c in range(GC):
                        a = g_z[:, c * CH:(c + 1) * CH]
                        last = act.activation(a, a, ACT.Exp, bias=g_row[:, 2:3], scale=-1.0,
                                              accum_out=g_sum[:, c:c + 1])
                    last.then_inc(g_exp, 1)
                    for c in range(GC):
                        act.wait_ge(g_tpsum, t * GC + (c + 1))
                        act.copy(g_adj[:, c * CH:(c + 1) * CH], turn_bank[c % 2][:]
                                 ).then_inc(g_turned, 1)

        @block.gpsimd
        def _(pool):
            for q in range(2):
                pool.sem_inc(p_lo[q], 1)
            pool.memset(ident[:], 0.0).then_inc(ident_ready, 1)
            pool.wait_ge(ident_ready, 1)
            pool.affine_select(out=ident[:], in_=ident[:], compare_op=ALU.not_equal, fill=1.0, base=0,
                               pattern=[[-1, P]], channel_multiplier=1).then_inc(ident_ready, 1)
            pool.memset(half[:], -0.5).then_inc(ident_ready, 1)
            pool.wait_ge(ident_ready, 3)
            pool.iota(ptr_drawn[:], pattern=[[GS, NG]], base=0, channel_multiplier=0
                      ).then_inc(ptr_id, 1)

            def root(count, q):
                pool.wait_ge(var_ready[q], count)
                pool.tensor_tensor(rstd[:, q:q + 1], var_eps[:, q:q + 1], half[:, 0:1], ALU.pow
                                   ).then_inc(rstd_ready[q], 1)

            with pool.If(regular_ptr(pool)):
                def root_two(u, q):
                    pool.wait_ge(p_var[q], u + 1)
                    pool.tensor_tensor(rstd_two[:, q, :], var_eps_two[:, q, :],
                                       half[:, 0:1].broadcast_to([P, 2]), ALU.pow
                                       ).then_inc(p_rstd[q], 1)

                def split_two(u, q):
                    at = bass.ds((u * 2 + q) * 2 * P, 2 * P)
                    pool.wait_ge(p_hi[q], u + 2)
                    pool.tensor_tensor(hT_lo[:, :, at], hT_two[q].rearrange("p (c d) -> p c d", c=KD),
                                       hT_hi[:, :, at].bitcast(F32), ALU.subtract).then_inc(p_lo[q], 1)

                for u in range(2):
                    root_two(u, 0)
                    root_two(u, 1)
                with pool.Fori(0, TWO - 2) as u:
                    for q in range(2):
                        split_two(u, q)
                        root_two(u + 2, q)
                pool.wait_ge(G_step, 2)
                pool.tensor_tensor(G_lo[:], G32[:], G_hi[:].bitcast(F32), ALU.subtract
                                   ).then_inc(G_step, 1)
                split_two(TWO - 2, 0)
                split_two(TWO - 2, 1)
                root(1, 0)
                split_two(TWO - 1, 0)
                split_two(TWO - 1, 1)

                def q_split(u, q, again):
                    twos = fixed(pool, u + 1)
                    products = fixed(pool, u * NC) if again and q == 1 else None
                    pool.wait_ge(ident_ready, 3)
                    pool.wait_ge(b_q32, twos)
                    if products is not None:
                        pool.wait_ge(b_spsum[1], products)
                    pool.tensor_scalar(Qb_hi[:, q], Qb32[:, q], 1.0, 0.0, ALU.mult, ALU.add
                                       ).then_inc(b_qhi[q], 1)
                    pool.wait_ge(b_qhi[q], u + 1)
                    pool.tensor_tensor(Qb_lo[:, q], Qb32[:, q], Qb_hi[:, q].bitcast(F32), ALU.subtract
                                       ).then_inc(b_q[q], 1)

                q_split(0, 0, False)

                def body(u, q, up, un):
                    if un is not None:
                        root(un + 1, 1 - q)
                    if q == 0:
                        q_split(u, 1, up is not None)
                    elif un is not None:
                        q_split(un, 0, True)
                    for c in range(NC):
                        pool.wait_ge(b_pT32[q], u * NC + (c + 1))
                        pool.tensor_tensor(PT_lo[:, c, :], PT32[:, c % 2, :],
                                           PT_hi[:, c, :].bitcast(F32), ALU.subtract).then_inc(b_pT[q], 1)

                alternate(pool, NT, body)
            with pool.Else():
                pool.iota(g_key_id, pattern=[[1, N]], base=0, channel_multiplier=0).then_inc(g_ids, 1)
                pool.iota(g_row_id[:], pattern=[[P, GT]], base=0, channel_multiplier=1
                          ).then_inc(g_ids, 1)
                with pool.Fori(0, GT) as t:
                    root(t + 1, 0)

        @block.vector
        def _(dve):
            for q in range(2):
                dve.sem_inc(p_vlo[q], 1)
                dve.sem_inc(s_out[q], 1)
                dve.sem_inc(b_out[q], 1)
                dve.sem_inc(s_stored[q], 16)
                dve.sem_inc(b_stored[q], 16)
            dve.wait_ge(ptr_in, 16)
            dve.wait_ge(ptr_id, 1)
            dve.tensor_tensor(ptr_same[:], ptr_row[:], ptr_drawn[:], ALU.is_equal).then_inc(ptr_step, 1)
            dve.wait_ge(ptr_step, 1)
            dve.tensor_reduce(path[:], ptr_same[:], AX.X, ALU.min).then_inc(path_known, 1)
            dve.memset(cap[:], -FAR).then_inc(const_ready, 1)
            dve.memset(floor[:], -BIG).then_inc(const_ready, 1)
            dve.wait_ge(const_ready, 2)
            for g in range(P // GS):
                s = slice(g * GS, (g + 1) * GS)
                dve.memset(cap[s, s], BIG)
                last = dve.memset(floor[s, s], FAR)
            last.then_inc(const_ready, 1)
            dve.wait_ge(const_ready, 3)
            dve.wait_ge(w_in, 6 * 16)
            for c in range(KD):
                last = dve.tensor_scalar(bq_wide[:, c, :], cap[:], 0.0, bq_col[:, c:c + 1], ALU.mult,
                                         ALU.add)
            last.then_inc(w_wide, 1)

            def take_u(steps):
                dve.wait_ge(prep_psum, 2)
                dve.wait_ge(G_step, steps)
                for i in range(KD):
                    dve.tensor_scalar(WvT[:, i, D:DU], G_bank[i][:, D:DU], SC, None, ALU.mult)
                dve.tensor_scalar(bias_row[:, D:DU], out_bank[:, 0:1], SC, None, ALU.mult
                                  ).then_inc(u_done, 1)

            def statistics(src, count, q):
                dve.bn_stats(moments[:, q, :], src).then_inc(moments_done[q], 1)
                count = fixed(dve, count)
                dve.wait_ge(const_ready, 3)
                dve.wait_ge(moments_done[q], count)
                dve.bn_aggr(mean_var[:, q, :], moments[:, q, :]).then_inc(mean_done[q], 1)
                dve.wait_ge(mean_done[q], count)
                dve.tensor_scalar(var_eps[:, q:q + 1], mean_var[:, q, 1:2], EPS, None, ALU.add
                                  ).then_inc(var_ready[q], 1)

            def normalize(src, count, q):
                dve.wait_ge(rstd_ready[q], count)
                dve.tensor_scalar(xn[:, q, :], src, mean_var[:, q, 0:1], rstd[:, q:q + 1],
                                  ALU.subtract, ALU.mult).then_inc(xn_ready[q], 1)

            with dve.If(regular_ptr(dve)):
                def stat_two(u, q):
                    for i in range(2):
                        last = dve.bn_stats(moments_two[:, q, i, :],
                                            x_big[:, bass.ds((u * 2 + q) * 2 + i, 1), :])
                    last.then_inc(p_moments[q], 1)
                    twos = fixed(dve, u + 1)
                    dve.wait_ge(const_ready, 3)
                    dve.wait_ge(p_moments[q], twos)
                    for i in range(2):
                        last = dve.bn_aggr(mean_var_two[:, q, i, :], moments_two[:, q, i, :])
                    last.then_inc(p_mean[q], 1)
                    dve.wait_ge(p_mean[q], twos)
                    dve.tensor_scalar(var_eps_two[:, q, :], mean_var_two[:, q, :, 1], EPS, None, ALU.add
                                      ).then_inc(p_var[q], 1)

                def normalize_two(u, q):
                    dve.wait_ge(p_rstd[q], u + 1)
                    for i in range(2):
                        n = (u * 2 + q) * 2 + i
                        last = dve.tensor_scalar(xn_two[q][:, i, :], x_big[:, n, :],
                                                 mean_var_two[:, q, i, 0:1], rstd_two[:, q, i:i + 1],
                                                 ALU.subtract, ALU.mult)
                    last.then_inc(p_xn[q], 1)

                def split_v(u, q):
                    n = (u * 2 + q) * 2
                    dve.wait_ge(p_vhi[q], u + 1)
                    for i in range(2):
                        dve.tensor_tensor(u_big[:, bass.ds(n + i, 1)], V_two_bank[q][i][:, D:DU],
                                          bias_row[:, D:DU], ALU.add)
                        last = dve.tensor_tensor(V_lo[:, n + i, :], V_two_bank[q][i][:, 0:D],
                                                 V_hi[:, n + i, :].bitcast(F32), ALU.subtract)
                    last.then_inc(p_vlo[q], 1)

                def off_big(u, q):
                    dve.wait_ge(adj_o_in[q], u * 16 + 16)
                    dve.tensor_scalar(adj_big[q][:, 0:H], adj_big[q][:, 0:H], OFF_SCALE, None, ALU.mult,
                                      ALU.min, accum_out=bound_b[:, q, 0:1]).then_inc(b_off[q], 1)
                    dve.wait_ge(b_off[q], u + 1)
                    dve.tensor_tensor(bound_b[:, q, 1:2], bound_b[:, q, 0:1],
                                      u_big[:, bass.ds(u * 2 + q, 1)], ALU.add).then_inc(b_offu[q], 1)

                def off_small(u, q, i):
                    a = adj_small[q][:, i * H:(i + 1) * H]
                    dve.tensor_scalar(a, a, OFF_SCALE, None, ALU.mult, ALU.min,
                                      accum_out=off_min[:, q, i:i + 1]).then_inc(s_off[q], 1)

                def mask_small(u, q):
                    block_cols = adj_small[q][:, bass.ds((u * 2 + q) * P, P)]
                    dve.wait_ge(adj_s_in[q], u * 32 + 32)
                    dve.tensor_tensor(diag[:, q, :], block_cols, cap[:], ALU.min).then_inc(s_diag[q], 1)
                    dve.wait_ge(s_diag[q], u + 1)
                    dve.tensor_tensor(block_cols, block_cols, floor[:], ALU.max).then_inc(s_masked[q], 1)
                    dve.wait_ge(s_masked[q], u + 1)
                    off_small(u, q, 0)

                dve.tensor_copy(bias_hi, bias_row[:, 0:D])
                dve.tensor_scalar(ones, cap[:], 0.0, 1.0, ALU.mult, ALU.add).then_inc(bias_step, 1)
                dve.wait_ge(bias_step, 1)
                dve.tensor_tensor(bias_lo, bias_row[:, 0:D], bias_hi.bitcast(F32), ALU.subtract
                                  ).then_inc(bias_step, 1)
                dve.wait_ge(x_in[0], 16)
                stat_two(0, 0)
                stat_two(0, 1)
                normalize_two(0, 0)
                normalize_two(0, 1)
                dve.wait_ge(x_in[1], 16)
                stat_two(1, 0)
                stat_two(1, 1)
                take_u(2)
                with dve.Fori(0, TWO - 2) as u:
                    for q in range(2):
                        dve.wait_ge(p_turned[q], u + 1)
                        normalize_two(u + 1, q)
                        stat_two(u + 2, q)
                        split_v(u, q)
                dve.wait_ge(p_turned[0], TWO - 1)
                normalize_two(TWO - 1, 0)
                split_v(TWO - 2, 0)
                dve.wait_ge(p_turned[1], TWO - 1)
                normalize_two(TWO - 1, 1)
                dve.wait_ge(p_vlo[0], 2)
                off_big(0, 0)
                split_v(TWO - 2, 1)
                dve.wait_ge(x_s_in[0], 16)
                statistics(x_small[:, 0, :], 1, 0)
                dve.wait_ge(p_turned[0], TWO)
                normalize(x_small[:, 0, :], 1, 0)
                mask_small(0, 0)
                off_small(0, 0, 1)
                split_v(TWO - 1, 0)
                split_v(TWO - 1, 1)
                dve.wait_ge(c_spread, 1)

                def scores(u, q, c):
                    products = fixed(dve, u * NC + (c + 1))
                    before = fixed(dve, u + 1 if c == 0 else u * NC + c)
                    landed = fixed(dve, u * 16 + 16) if c == 0 else None
                    dve.wait_ge(const_ready, 3)
                    if c == 0:
                        dve.wait_ge(adj_b_in[q], landed)
                    dve.wait_ge(b_spsum[q], products)
                    dve.wait_ge(b_offu[q] if c == 0 else b_scores[q], before)
                    a = adj_big[q][:, H + c * CH:H + (c + 1) * CH]
                    dve.tensor_tensor_reduce(a, score_bank[c % 3][:], a, -2.0, bound_b[:, q, 1 + c:2 + c],
                                             ALU.add, ALU.min, bound_b[:, q, 2 + c:3 + c]
                                             ).then_inc(b_scores[q], 1)

                def out_big(u, q):
                    dve.wait_ge(adj_b_free[q], u + 2)
                    dve.tensor_reduce(sum_b[:, q, 3:4], sum_b[:, q, 0:3], AX.X, ALU.add
                                      ).then_inc(b_total[q], 1)
                    dve.wait_ge(b_total[q], u + 1)
                    dve.reciprocal(sum_b[:, q, 4:5], sum_b[:, q, 3:4]).then_inc(b_recip[q], 1)
                    dve.wait_ge(b_recip[q], u + 1)
                    dve.wait_ge(b_stored[q], u * 16 + 16)
                    dve.wait_ge(b_pv[q], u * NC + NC)
                    dve.scalar_tensor_tensor(out=out_b[:, q, :], in0=out_bank[:, 0:D],
                                             scalar=sum_b[:, q, 4:5], in1=x_big[:, u * 2 + q, :],
                                             op0=ALU.mult, op1=ALU.add).then_inc(b_out[q], 1)

                def out_small(u, q):
                    dve.wait_ge(adj_s_free[1][q], u + 2)
                    dve.tensor_reduce(sum_s[:, q, 3:4], sum_s[:, q, 0:3], AX.X, ALU.add
                                      ).then_inc(s_total[q], 1)
                    dve.wait_ge(s_total[q], u + 1)
                    dve.reciprocal(sum_s[:, q, 4:5], sum_s[:, q, 3:4]).then_inc(s_recip[q], 1)
                    dve.wait_ge(s_recip[q], u + 1)
                    dve.wait_ge(s_stored[q], u * 16 + 16)
                    dve.wait_ge(x_s_in[q], u * 16 + 16)
                    dve.wait_ge(s_opsum[q], u + 1)
                    dve.scalar_tensor_tensor(out=out_s[:, q, :], in0=small_bank[:, 0:D],
                                             scalar=sum_s[:, q, 4:5], in1=x_small[:, q, :],
                                             op0=ALU.mult, op1=ALU.add).then_inc(s_out[q], 1)

                def front(u, q):
                    dve.wait_ge(s_qpsum[q], u + 1)
                    dve.tensor_tensor(Qs[:, q].rearrange("p c d -> p (c d)"), query_bank[:, 0:KD * P],
                                      c_wide[:].rearrange("p c d -> p (c d)"), ALU.add
                                      ).then_inc(s_q[q], 1)
                    dve.wait_ge(s_vpsum[q], u + 1)
                    dve.tensor_tensor(V32[:, q, :], score_bank[2][:, 0:DU], bias_row[:], ALU.add
                                      ).then_inc(s_v[q], 1)
                    scores(u, q, 0)
                    scores(u, q, 1)
                    dve.wait_ge(s_off[q], u * 2 + 2)
                    dve.scalar_tensor_tensor(out=bound_s[:, q, 0:1], in0=off_min[:, q, 0:1],
                                             scalar=off_min[:, q, 1:2], in1=V32[:, q, D:DU],
                                             op0=ALU.min, op1=ALU.add).then_inc(s_offu[q], 1)
                    tiles = fixed(dve, u + 1)
                    dve.wait_ge(const_ready, 3)
                    dve.wait_ge(s_offu[q], tiles)
                    dve.wait_ge(s_spsum[q], tiles)
                    dve.tensor_tensor_reduce(diag[:, q, :], small_bank[:, 0:P], diag[:, q, :], -2.0,
                                             bound_s[:, q, 0:1], ALU.add, ALU.min, bound_s[:, q, 1:2]
                                             ).then_inc(s_bound[q], 1)
                    dve.wait_ge(s_bound[q], u + 1)
                    dve.tensor_tensor(bound_s[:, q, 2:3], bound_s[:, q, 1:2], V32[:, q, D:DU],
                                      ALU.subtract).then_inc(s_stat[q], 1)

                front(0, 0)

                def body(u, q, up, un):
                    if un is not None:
                        dve.wait_ge(x_s_in[1 - q], un * 16 + 16)
                        statistics(x_small[:, 1 - q, :], un + 1, 1 - q)
                    scores(u, q, 2)
                    scores(u, q, 3)
                    dve.wait_ge(b_scores[q], u * NC + NC)
                    dve.tensor_tensor(bound_b[:, q, 6:7], bound_b[:, q, 5:6],
                                      u_big[:, bass.ds(u * 2 + q, 1)], ALU.subtract
                                      ).then_inc(b_stat[q], 1)
                    if un is not None:
                        normalize(x_small[:, 1 - q, :], un + 1, 1 - q)
                        off_big(un, 1 - q)
                        mask_small(un, 1 - q)
                        off_small(un, 1 - q, 1)
                        out_small(u, q)
                        front(un, 1 - q)
                    if up is not None:
                        out_big(up, 1 - q)
                    if un is None:
                        out_small(u, q)

                alternate(dve, NT, body)
                out_big(LAST, 1)
            with dve.Else():
                take_u(1)
                dve.wait_ge(c_spread, 1)
                dve.wait_ge(g_ids, 2)
                dve.tensor_copy(g_ptr[:], ptr_row[:])
                dve.memset(g_graph[:], 0.0)
                dve.memset(g_rows[:], 0.0).then_inc(g_clear, 1)
                dve.wait_ge(g_clear, 1)
                with dve.Fori(0, NG) as i:
                    edge = g_ptr[:, bass.ds(i, 1)]
                    dve.scalar_tensor_tensor(out=g_graph[:], in0=g_key_id, scalar=edge, in1=g_graph[:],
                                             op0=ALU.is_ge, op1=ALU.add)
                    dve.scalar_tensor_tensor(out=g_rows[:], in0=g_row_id[:], scalar=edge,
                                             in1=g_rows[:], op0=ALU.is_ge, op1=ALU.add
                                             ).then_inc(g_clear, 1)
                    dve.wait_ge(g_clear, i + 2)

                with dve.Fori(0, GT) as t:
                    dve.wait_ge(x_s_in[0], t * 16 + 16)
                    statistics(x_small[:, 0, :], t + 1, 0)
                    normalize(x_small[:, 0, :], t + 1, 0)
                    dve.wait_ge(s_vpsum[0], t + 1)
                    dve.tensor_tensor(g_V[:, t, :], query_bank[:, 0:DU], bias_row[:], ALU.add
                                      ).then_inc(s_v[0], 1)
                dve.wait_ge(s_v[0], GT)
                dve.sem_inc(g_graphs, 1)

                with dve.Fori(0, GT) as t:
                    steps = [0]

                    def step(ins):
                        ins.then_inc(g_step, 1)
                        steps[0] += 1
                        dve.wait_ge(g_step, t * G_STEPS + steps[0])

                    dve.wait_ge(s_qpsum[0], t + 1)
                    dve.tensor_tensor(Qs[:, 0].rearrange("p c d -> p (c d)"), query_bank[:, 0:KD * P],
                                      c_wide[:].rearrange("p c d -> p (c d)"), ALU.add
                                      ).then_inc(s_q[0], 1)
                    step(dve.tensor_copy(g_row[:, 0:1], g_rows[:, bass.ds(t, 1)]))
                    step(dve.tensor_copy(g_row[:, 1:2], g_V[:, t, D:DU]))
                    step(dve.tensor_scalar(g_in[:], g_graph[:], g_row[:, 0:1], 2 * FARTHEST,
                                           ALU.is_equal, ALU.mult))
                    step(dve.tensor_scalar(g_in[:], g_in[:], -FARTHEST, None, ALU.add))
                    dve.wait_ge(g_adj_in, t * 16 + 16)
                    step(dve.tensor_scalar(g_z[:], g_adj[:], OFF_SCALE, g_row[:, 1:2], ALU.mult,
                                           ALU.add))
                    step(dve.scalar_tensor_tensor(out=g_z[:], in0=g_in[:], scalar=-1.0, in1=g_z[:],
                                                  op0=ALU.mult, op1=ALU.min))
                    for c in range(GC):
                        dve.wait_ge(g_spsum, t * GC + (c + 1))
                        a = g_adj[:, c * CH:(c + 1) * CH]
                        step(dve.tensor_tensor(a, score_bank[c % 2][:], a, ALU.add))
                    step(dve.scalar_tensor_tensor(out=g_adj[:], in0=g_adj[:], scalar=-2.0,
                                                  in1=g_in[:], op0=ALU.mult, op1=ALU.min))
                    step(dve.tensor_tensor(g_z[:], g_z[:], g_adj[:], ALU.max))
                    step(dve.tensor_reduce(g_row[:, 2:3], g_z[:], AX.X, ALU.min))
                    assert steps[0] == G_BOUND
                    dve.wait_ge(g_exp, t + 1)
                    step(dve.scalar_tensor_tensor(out=g_z[:], in0=g_in[:], scalar=0.0, in1=g_z[:],
                                                  op0=ALU.is_gt, op1=ALU.mult))
                    step(dve.tensor_reduce(g_sum[:, GC:GC + 1], g_sum[:, 0:GC], AX.X, ALU.add))
                    step(dve.reciprocal(g_sum[:, GC + 1:GC + 2], g_sum[:, GC:GC + 1]))
                    dve.wait_ge(g_opsum, t + 1)
                    dve.wait_ge(g_x_in, t * 16 + 16)
                    step(dve.tensor_scalar(out_s[:, 0, :], out_bank[:, 0:D],
                                           g_sum[:, GC + 1:GC + 2], None, ALU.mult))
                    step(dve.tensor_tensor(out_s[:, 0, :], out_s[:, 0, :], x_small[:, 1, :], ALU.add))
                    assert steps[0] == G_STEPS
                    dve.sem_inc(g_out, 1)

        @block.tensor
        def _(pe):
            pe.wait_ge(w_in, 6 * 16)
            pe.wait_ge(ident_ready, 2)
            for i in range(KD):
                for o in range(KD):
                    last = pe.transpose(query_bank[:, i * D + o * P:i * D + (o + 1) * P],
                                        Wv_sb[:, o, i * P:(i + 1) * P], ident[:])
            last.then_inc(prep_psum, 1)
            pe.wait_ge(w_wide, 1)
            for o in range(KD):
                last = pe.matmul(out_bank[:, 0:1], bq_wide[:, o, :], Wk_bk[:, o, D:DU],
                                 start=(o == 0), stop=(o == KD - 1))
            last.then_inc(prep_psum, 1)
            pe.wait_ge(wvt_done, 1)
            for i in range(KD):
                for o in range(KD):
                    last = pe.matmul(query_bank[:, i:i + 1], Wk_bk[:, o, i * P:(i + 1) * P],
                                     bq_col[:, o:o + 1], start=(o == 0), stop=(o == KD - 1))
            last.then_inc(G_psum, 1)
            for i in range(KD):
                for o in range(KD):
                    last = pe.matmul(G_bank[i][:, 0:DU], Wq_sb[:, o, i * P:(i + 1) * P],
                                     Wk_bk[:, o, :], start=(o == 0), stop=(o == KD - 1))
            last.then_inc(G_psum, 1)

            def turn(bank, q, done):
                for c in range(KD):
                    last = pe.transpose(bank[:, c * P:(c + 1) * P], xn[:, q, c * P:(c + 1) * P],
                                        ident[:])
                last.then_inc(done[q], 1)

            def project_v(bank, q, done):
                for c in range(KD):
                    last = pe.matmul(bank[:, 0:DU], hT[:, q, c, :], WvT[:, c, :], start=(c == 0),
                                     stop=(c == KD - 1))
                last.then_inc(done[q], 1)

            with pe.If(regular_ptr(pe)):
                def turn_big(u, q):
                    pe.wait_ge(p_hi[q], u + 1)
                    pe.wait_ge(p_xn[q], u + 1)
                    for c in range(KD):
                        for i in range(2):
                            last = pe.transpose(score_bank[q][:, (c * 2 + i) * P:(c * 2 + i + 1) * P],
                                                xn_two[q][:, i, c * P:(c + 1) * P], ident[:])
                    last.then_inc(p_turned[q], 1)

                def q_big(u):
                    for j in range(KD):
                        k = 0
                        for c in range(KD):
                            for g, h in ((G_hi, hT_hi), (G_hi, hT_lo), (G_lo, hT_hi)):
                                last = pe.matmul(query_bank[:, j * 2 * P:(j + 1) * 2 * P],
                                                 g[:, c, j * P:(j + 1) * P],
                                                 h[:, c, bass.ds(u * 2 * P, 2 * P)], start=(k == 0),
                                                 stop=(k == 3 * KD - 1))
                                k += 1
                    last.then_inc(b_qpsum, 1)

                def before(u, q, up, un):
                    if un is not None:
                        turn_big(un, 1 - q)
                    else:
                        pe.wait_ge(G_step, 3)
                        pe.wait_ge(p_lo[0], 2)
                        q_big(0)
                    pe.wait_ge(p_vlo[q], u + 1)
                    if q == 1:
                        pe.wait_ge(G_step, 2)
                    if up is None:
                        pe.wait_ge(u_done, 1)
                        pe.wait_ge(bias_step, 2)
                    pe.wait_ge(p_h32[q], u + 1)
                    for i in range(2):
                        for c in range(KD):
                            last = pe.matmul(V_two_bank[q][i][:, 0:DU],
                                             hT_two[q][:, (c * 2 + i) * P:(c * 2 + i + 1) * P],
                                             WvT[:, c, :], start=(c == 0), stop=(c == KD - 1))
                            if c == 0:
                                for b in (bias_hi, bias_lo):
                                    pe.matmul(V_two_bank[q][i][:, 0:D], ones[0:1, :], b[0:1, :],
                                              start=False, stop=False)
                    last.then_inc(p_vpsum[q], 1)

                turn_big(0, 0)
                alternate(pe, NT // 2, before)

                pe.wait_ge(b_q32, 1)
                pe.wait_ge(xn_ready[0], 1)
                turn(query_bank, 0, s_turned)

                def score_chunk(u, q, c):
                    if c == 3:
                        pe.wait_ge(b_scores[q], u * NC + 1)
                    k = 0
                    for j in range(KD):
                        for a, h in ((Qb_hi, hT_hi), (Qb_hi, hT_lo), (Qb_lo, hT_hi)):
                            last = pe.matmul(score_bank[c % 3][:], a[:, q, j, :],
                                             h[:, j, c * CH:(c + 1) * CH], start=(k == 0),
                                             stop=(k == 3 * KD - 1))
                            k += 1
                    last.then_inc(b_spsum[q], 1)

                def turn_probs(u, q, c):
                    pe.wait_ge(b_probs[q], u * 2 + (2 + c // 2))
                    if c >= 2:
                        pe.wait_ge(b_pT32[q], u * NC + (c - 1))
                    for k in range(KB):
                        last = pe.transpose(turn_bank[c % 2][:, k * P:(k + 1) * P],
                                            probs[:, (c * KB + k) * P:(c * KB + k + 1) * P], ident[:])
                    last.then_inc(b_tpsum[q], 1)

                def attend(u, q, c):
                    pe.wait_ge(b_pT[q], u * NC + (c + 1))
                    for k in range(KB):
                        b = c * KB + k
                        s = slice(k * P, (k + 1) * P)
                        for i, (a, v) in enumerate(((PT_hi, V_hi), (PT_hi, V_lo), (PT_lo, V_hi))):
                            last = pe.matmul(out_bank[:, 0:D], a[:, c, s], v[:, b, :],
                                             start=(b == 0 and i == 0), stop=(b == NT - 1 and i == 2))
                    last.then_inc(b_pv[q], 1)

                def q_small(u, q):
                    pe.wait_ge(s_hT[q], u + 1)
                    for j in range(KD):
                        for c in range(KD):
                            last = pe.matmul(query_bank[:, j * P:(j + 1) * P],
                                             G32[:, c, j * P:(j + 1) * P], hT[:, q, c, :],
                                             start=(c == 0), stop=(c == KD - 1))
                    last.then_inc(s_qpsum[q], 1)

                q_small(0, 0)
                for i in range(2):
                    pe.wait_ge(p_lo[i], TWO + 1)

                def body(u, q, up, un):
                    pe.wait_ge(b_q[q], u + 1)
                    if up is not None:
                        pe.wait_ge(b_scores[1 - q], up * NC + NC)
                    score_chunk(u, q, 0)
                    project_v(score_bank[2], q, s_vpsum)
                    score_chunk(u, q, 1)
                    if up is not None:
                        pe.wait_ge(s_out[1 - q], up + 2)
                    else:
                        for i in range(2):
                            pe.wait_ge(p_vlo[i], TWO + 1)
                    pe.wait_ge(s_q[q], u + 1)
                    pe.wait_ge(s_v[q], u + 1)
                    for c in range(KD):
                        last = pe.matmul(small_bank[:, 0:P], Qs[:, q, c, :], hT[:, q, c, :],
                                         start=(c == 0), stop=(c == KD - 1))
                    last.then_inc(s_spsum[q], 1)
                    if q == 1 and un is not None:
                        q_big(un)
                    score_chunk(u, q, 2)
                    score_chunk(u, q, 3)
                    pe.wait_ge(s_probs[q], u + 1)
                    if q == 1 and un is not None:
                        pe.wait_ge(b_q32, un + 1)
                    pe.transpose(query_bank[:, 0:P], diag[:, q, :], ident[:]).then_inc(s_tpsum[q], 1)
                    if up is not None:
                        pe.wait_ge(b_out[q], u + 1)
                        attend(up, 1 - q, 0)
                        attend(up, 1 - q, 1)
                    pe.wait_ge(s_pT[q], u + 1)
                    pe.wait_ge(s_stat[q], u + 1)
                    pe.matmul(small_bank[:, 0:D], PsT[:, q, :], V32[:, q, 0:D], start=True, stop=True
                              ).then_inc(s_opsum[q], 1)
                    if un is not None:
                        pe.wait_ge(xn_ready[1 - q], un + 1)
                        turn(query_bank, 1 - q, s_turned)
                    for c in range(NC):
                        turn_probs(u, q, c)
                        if c == 1:
                            if up is not None:
                                attend(up, 1 - q, 2)
                                attend(up, 1 - q, 3)
                            if un is not None:
                                q_small(un, 1 - q)

                alternate(pe, NT, body)
                pe.wait_ge(b_out[0], LAST + 2)
                for c in range(NC):
                    attend(LAST, 1, c)
            with pe.Else():
                pe.wait_ge(G_step, 1)
                pe.wait_ge(c_spread, 1)
                pe.wait_ge(u_done, 1)
                with pe.Fori(0, GT) as t:
                    pe.wait_ge(xn_ready[0], t + 1)
                    turn(small_bank, 0, s_turned)
                    pe.wait_ge(s_hT[0], t + 1)
                    project_v(query_bank, 0, s_vpsum)
                    pe.wait_ge(s_v[0], t + 1)
                with pe.Fori(0, GT) as t:
                    for j in range(KD):
                        for c in range(KD):
                            last = pe.matmul(query_bank[:, j * P:(j + 1) * P],
                                             G32[:, c, j * P:(j + 1) * P],
                                             g_hT[:, c, bass.ds(t * P, P)], start=(c == 0),
                                             stop=(c == KD - 1))
                    last.then_inc(s_qpsum[0], 1)
                    pe.wait_ge(s_q[0], t + 1)
                    for c in range(GC):
                        if c >= 2:
                            pe.wait_ge(g_step, t * G_STEPS + (5 + c))
                        for j in range(KD):
                            last = pe.matmul(score_bank[c % 2][:], Qs[:, 0, j, :],
                                             g_hT[:, j, c * CH:(c + 1) * CH], start=(j == 0),
                                             stop=(j == KD - 1))
                        last.then_inc(g_spsum, 1)
                    pe.wait_ge(g_step, t * G_STEPS + (G_BOUND + 1))
                    for c in range(GC):
                        if c >= 2:
                            pe.wait_ge(g_turned, t * GC + (c - 1))
                        for k in range(KB):
                            b = c * KB + k
                            last = pe.transpose(turn_bank[c % 2][:, k * P:(k + 1) * P],
                                                g_z[:, b * P:(b + 1) * P], ident[:])
                        last.then_inc(g_tpsum, 1)
                    pe.wait_ge(g_turned, t * GC + GC)
                    for b in range(GT):
                        last = pe.matmul(out_bank[:, 0:D], g_adj[:, b * P:(b + 1) * P],
                                         g_V[:, b, 0:D], start=(b == 0), stop=(b == GT - 1))
                    last.then_inc(g_opsum, 1)
                    pe.wait_ge(g_out, t + 1)


_INS = ['x', 'adj', 'L0_gnn_ptr', 'L0_gnn_Wq', 'L0_gnn_bq', 'L0_gnn_Wk', 'L0_gnn_bk', 'L0_gnn_Wv', 'L0_gnn_bv']


def kernel(**inputs):
    import numpy as _np
    import concourse.bacc as _bacc
    from concourse import mybir as _mybir
    from concourse.bass_utils import run_bass_kernel_spmd as _run

    nc = _bacc.Bacc("TRN2", target_bir_lowering=False, num_devices=1)
    arrays, args = {}, []
    for name in _INS:
        a = _np.ascontiguousarray(inputs[name])
        arrays[f"in_{name}"] = a
        args.append(nc.dram_tensor(f"in_{name}", a.shape, _mybir.dt.from_np(a.dtype), kind="ExternalInput").ap())
    shape = inputs['x'].shape
    args.append(nc.dram_tensor("out_0", shape, _mybir.dt.float32, kind="ExternalOutput").ap())
    build_program(nc, *args)
    r = _run(nc, [arrays], core_ids=[0])
    return r.results[0]["out_0"]
```
